# Optimizing a Trainium2 kernel written in Bass

```python
import numpy as np
import jax
import jax.numpy as jnp

def _softmax(x, axis=-1):
    return jax.nn.softmax(x, axis=axis)

def _gelu(x):
    return jax.nn.gelu(x, approximate=True)

def _silu(x):
    return jax.nn.silu(x)

def _sigmoid(x):
    return jax.nn.sigmoid(x)

def _layernorm(x, axis=-1, eps=1e-05):
    m = jnp.mean(x, axis=axis, keepdims=True)
    v = jnp.var(x, axis=axis, keepdims=True)
    return (x - m) / jnp.sqrt(v + eps)

def _scatter_add(tgt, idx, src, axis=0):
    return tgt.at[idx].add(src)

def _segment_sum(src, seg, n):
    return jax.ops.segment_sum(src, seg, n)
kernel_name = 'mk_seq_postln_d1_jaxref_r4_970e31'

def setup_inputs(seed: int=0):
    np.random.seed(seed)
    _w = jnp.asarray

    def _L0_attn_setup():
        import jax, jax.numpy as jnp
        import numpy as np
        EPS = 1e-06

        def elu_feature_map(x):
            return jax.nn.elu(x) + 1.0
        key = jax.random.key(seed)
        ks = jax.random.split(key, 5)
        B, S, D, H, Hd = (4, 1024, 256, 16, 64)
        scale = 1.0 / np.sqrt(D)
        x = jax.random.normal(ks[0], (B, S, D), dtype=jnp.float32)
        Wq = jax.random.normal(ks[1], (D, H, Hd), dtype=jnp.float32) * scale
        Wk = jax.random.normal(ks[2], (D, H, Hd), dtype=jnp.float32) * scale
        Wv = jax.random.normal(ks[3], (D, H, Hd), dtype=jnp.float32) * scale
        Wo = jax.random.normal(ks[4], (H, Hd, D), dtype=jnp.float32) * (1.0 / np.sqrt(H * Hd))
        bq = jnp.zeros((H, Hd), dtype=jnp.float32)
        bk = jnp.zeros((H, Hd), dtype=jnp.float32)
        bv = jnp.zeros((H, Hd), dtype=jnp.float32)
        bo = jnp.zeros((D,), dtype=jnp.float32)
        return {'x': x, 'Wq': Wq, 'bq': bq, 'Wk': Wk, 'bk': bk, 'Wv': Wv, 'bv': bv, 'Wo': Wo, 'bo': bo}
    _L0_attn_in = _L0_attn_setup()

    def _L0_ffn_setup():
        import jax, jax.numpy as jnp
        import numpy as np
        H = 256
        NH = 16
        HD = H // NH
        HH = HD // 2
        L = H // 4
        I = int(H * 1.0)
        ER = 7
        TOPK = 2
        BASE = 10000.0
        EPS = 1e-05

        def rmsnorm(x, w):
            norm = jnp.sqrt(jnp.mean(x * x, axis=-1, keepdims=True)) + EPS
            return x / norm * w

        def rope_tables(seq_len):
            inv_freq = 1.0 / BASE ** (jnp.arange(0, HH, 2, dtype=jnp.float32) / HH)
            t = jnp.arange(seq_len, dtype=jnp.float32)
            freqs = jnp.einsum('i,j->ij', t, inv_freq)
            emb = jnp.concatenate([freqs, freqs], axis=-1)
            cos = jnp.cos(emb)[None, :, None, :]
            sin = jnp.sin(emb)[None, :, None, :]
            return (cos, sin)

        def rotate_half(x):
            x1, x2 = jnp.split(x, 2, axis=-1)
            return jnp.concatenate([-x2, x1], axis=-1)

        def silu(x):
            return x * jax.nn.sigmoid(x)

        def mla(xn, W_kvd, W_qd, W_ku, W_qu, W_vu, W_ropeq, W_ropek, W_o):
            B, S, _ = xn.shape
            kv_lat = xn @ W_kvd
            q_lat = xn @ W_qd
            k = (kv_lat @ W_ku).reshape(B, S, NH, HH)
            q = (q_lat @ W_qu).reshape(B, S, NH, HH)
            v = (kv_lat @ W_vu).reshape(B, S, NH, HD)
            q_rope = (q_lat @ W_ropeq).reshape(B, S, NH, HH)
            k_rope = (xn @ W_ropek).reshape(B, S, NH, HH)
            cos, sin = rope_tables(S)
            k_rope = k_rope * cos + rotate_half(k_rope) * sin
            q_rope = q_rope * cos + rotate_half(q_rope) * sin
            kk = jnp.concatenate([k, k_rope], axis=-1)
            qq = jnp.concatenate([q, q_rope], axis=-1)
            scale = 1.0 / jnp.sqrt(jnp.float32(HD))
            scores = jnp.einsum('bqhd,bkhd->bhqk', qq, kk) * scale
            causal = jnp.tril(jnp.ones((S, S), dtype=bool))
            scores = jnp.where(causal[None, None], scores, jnp.finfo(scores.dtype).min)
            probs = jax.nn.softmax(scores, axis=-1)
            y = jnp.einsum('bhqk,bkhd->bqhd', probs, v).reshape(B, S, H)
            return y @ W_o

        def moe(xn, Wg_s, Wu_s, Wd_s, Wg_r, Wu_r, Wd_r, W_router, routing_bias):
            B, S, _ = xn.shape
            xt = xn.reshape(B * S, H)
            shared = silu(xt @ Wg_s) * (xt @ Wu_s) @ Wd_s
            logits = xt @ W_router + routing_bias
            probs = jax.nn.sigmoid(logits)
            scores, idx = jax.lax.top_k(probs, TOPK)
            scores = scores / jnp.sum(scores, axis=-1, keepdims=True)
            wts = jnp.sum(jax.nn.one_hot(idx, ER, dtype=xt.dtype) * scores[..., None], axis=1)
            g = jnp.einsum('th,ehi->tei', xt, Wg_r)
            u = jnp.einsum('th,ehi->tei', xt, Wu_r)
            hmid = silu(g) * u
            combined = jnp.einsum('tei,eih,te->th', hmid, Wd_r, wts)
            return (shared + combined).reshape(B, S, H)
        key = jax.random.key(seed)
        ks = jax.random.split(key, 20)
        s = 0.02
        r = lambda k, shp: jax.random.normal(k, shp, dtype=jnp.float32) * s
        return {'x': jax.random.normal(ks[0], (4, 256, H), dtype=jnp.float32), 'w_ln1': jnp.ones((H,), jnp.float32), 'w_ln2': jnp.ones((H,), jnp.float32), 'W_kvd': r(ks[1], (H, L)), 'W_qd': r(ks[2], (H, L)), 'W_ku': r(ks[3], (L, NH * HH)), 'W_qu': r(ks[4], (L, NH * HH)), 'W_vu': r(ks[5], (L, H)), 'W_ropeq': r(ks[6], (L, H // 2)), 'W_ropek': r(ks[7], (H, H // 2)), 'W_o': r(ks[8], (H, H)), 'Wg_s': r(ks[9], (H, I)), 'Wu_s': r(ks[10], (H, I)), 'Wd_s': r(ks[11], (I, H)), 'Wg_r': r(ks[12], (ER, H, I)), 'Wu_r': r(ks[13], (ER, H, I)), 'Wd_r': r(ks[14], (ER, I, H)), 'W_router': r(ks[15], (H, ER)), 'routing_bias': jnp.zeros((ER,), jnp.float32)}
    _L0_ffn_in = _L0_ffn_setup()
    _d = {'L0_attn_x': _L0_attn_in['x'], 'L0_attn_Wq': _L0_attn_in['Wq'], 'L0_attn_bq': _L0_attn_in['bq'], 'L0_attn_Wk': _L0_attn_in['Wk'], 'L0_attn_bk': _L0_attn_in['bk'], 'L0_attn_Wv': _L0_attn_in['Wv'], 'L0_attn_bv': _L0_attn_in['bv'], 'L0_attn_Wo': _L0_attn_in['Wo'], 'L0_attn_bo': _L0_attn_in['bo'], 'L0_ffn_w_ln1': _L0_ffn_in['w_ln1'], 'L0_ffn_w_ln2': _L0_ffn_in['w_ln2'], 'L0_ffn_W_kvd': _L0_ffn_in['W_kvd'], 'L0_ffn_W_qd': _L0_ffn_in['W_qd'], 'L0_ffn_W_ku': _L0_ffn_in['W_ku'], 'L0_ffn_W_qu': _L0_ffn_in['W_qu'], 'L0_ffn_W_vu': _L0_ffn_in['W_vu'], 'L0_ffn_W_ropeq': _L0_ffn_in['W_ropeq'], 'L0_ffn_W_ropek': _L0_ffn_in['W_ropek'], 'L0_ffn_W_o': _L0_ffn_in['W_o'], 'L0_ffn_Wg_s': _L0_ffn_in['Wg_s'], 'L0_ffn_Wu_s': _L0_ffn_in['Wu_s'], 'L0_ffn_Wd_s': _L0_ffn_in['Wd_s'], 'L0_ffn_Wg_r': _L0_ffn_in['Wg_r'], 'L0_ffn_Wu_r': _L0_ffn_in['Wu_r'], 'L0_ffn_Wd_r': _L0_ffn_in['Wd_r'], 'L0_ffn_W_router': _L0_ffn_in['W_router'], 'L0_ffn_routing_bias': _L0_ffn_in['routing_bias']}
    _x0 = _d['L0_attn_x']
    _d['L0_attn_x'] = jax.random.normal(jax.random.fold_in(jax.random.key(seed), 1), (4, 1024, 256), dtype=_x0.dtype)
    del _x0
    return _d

def reference(L0_attn_x, L0_attn_Wq, L0_attn_bq, L0_attn_Wk, L0_attn_bk, L0_attn_Wv, L0_attn_bv, L0_attn_Wo, L0_attn_bo, L0_ffn_w_ln1, L0_ffn_w_ln2, L0_ffn_W_kvd, L0_ffn_W_qd, L0_ffn_W_ku, L0_ffn_W_qu, L0_ffn_W_vu, L0_ffn_W_ropeq, L0_ffn_W_ropek, L0_ffn_W_o, L0_ffn_Wg_s, L0_ffn_Wu_s, L0_ffn_Wd_s, L0_ffn_Wg_r, L0_ffn_Wu_r, L0_ffn_Wd_r, L0_ffn_W_router, L0_ffn_routing_bias):

    def _L0_attn_ref(x, Wq, bq, Wk, bk, Wv, bv, Wo, bo):
        import jax, jax.numpy as jnp
        import numpy as np
        EPS = 1e-06

        def elu_feature_map(x):
            return jax.nn.elu(x) + 1.0
        q = jnp.einsum('nsD,Dhd->nshd', x, Wq) + bq
        k = jnp.einsum('nsD,Dhd->nshd', x, Wk) + bk
        v = jnp.einsum('nsD,Dhd->nshd', x, Wv) + bv
        qf = elu_feature_map(q)
        kf = elu_feature_map(k)
        kv = jnp.einsum('nshd,nshm->nhmd', kf, v)
        z = 1.0 / (jnp.einsum('nlhd,nhd->nlh', qf, jnp.sum(kf, axis=1)) + EPS)
        y = jnp.einsum('nlhd,nhmd,nlh->nlhm', qf, kv, z)
        out = jnp.einsum('nlhm,hmD->nlD', y, Wo) + bo
        return out

    def _L0_ffn_ref(x, w_ln1, w_ln2, W_kvd, W_qd, W_ku, W_qu, W_vu, W_ropeq, W_ropek, W_o, Wg_s, Wu_s, Wd_s, Wg_r, Wu_r, Wd_r, W_router, routing_bias):
        import jax, jax.numpy as jnp
        import numpy as np
        H = 256
        NH = 16
        HD = H // NH
        HH = HD // 2
        L = H // 4
        I = int(H * 1.0)
        ER = 7
        TOPK = 2
        BASE = 10000.0
        EPS = 1e-05

        def rmsnorm(x, w):
            norm = jnp.sqrt(jnp.mean(x * x, axis=-1, keepdims=True)) + EPS
            return x / norm * w

        def rope_tables(seq_len):
            inv_freq = 1.0 / BASE ** (jnp.arange(0, HH, 2, dtype=jnp.float32) / HH)
            t = jnp.arange(seq_len, dtype=jnp.float32)
            freqs = jnp.einsum('i,j->ij', t, inv_freq)
            emb = jnp.concatenate([freqs, freqs], axis=-1)
            cos = jnp.cos(emb)[None, :, None, :]
            sin = jnp.sin(emb)[None, :, None, :]
            return (cos, sin)

        def rotate_half(x):
            x1, x2 = jnp.split(x, 2, axis=-1)
            return jnp.concatenate([-x2, x1], axis=-1)

        def silu(x):
            return x * jax.nn.sigmoid(x)

        def mla(xn, W_kvd, W_qd, W_ku, W_qu, W_vu, W_ropeq, W_ropek, W_o):
            B, S, _ = xn.shape
            kv_lat = xn @ W_kvd
            q_lat = xn @ W_qd
            k = (kv_lat @ W_ku).reshape(B, S, NH, HH)
            q = (q_lat @ W_qu).reshape(B, S, NH, HH)
            v = (kv_lat @ W_vu).reshape(B, S, NH, HD)
            q_rope = (q_lat @ W_ropeq).reshape(B, S, NH, HH)
            k_rope = (xn @ W_ropek).reshape(B, S, NH, HH)
            cos, sin = rope_tables(S)
            k_rope = k_rope * cos + rotate_half(k_rope) * sin
            q_rope = q_rope * cos + rotate_half(q_rope) * sin
            kk = jnp.concatenate([k, k_rope], axis=-1)
            qq = jnp.concatenate([q, q_rope], axis=-1)
            scale = 1.0 / jnp.sqrt(jnp.float32(HD))
            scores = jnp.einsum('bqhd,bkhd->bhqk', qq, kk) * scale
            causal = jnp.tril(jnp.ones((S, S), dtype=bool))
            scores = jnp.where(causal[None, None], scores, jnp.finfo(scores.dtype).min)
            probs = jax.nn.softmax(scores, axis=-1)
            y = jnp.einsum('bhqk,bkhd->bqhd', probs, v).reshape(B, S, H)
            return y @ W_o

        def moe(xn, Wg_s, Wu_s, Wd_s, Wg_r, Wu_r, Wd_r, W_router, routing_bias):
            B, S, _ = xn.shape
            xt = xn.reshape(B * S, H)
            shared = silu(xt @ Wg_s) * (xt @ Wu_s) @ Wd_s
            logits = xt @ W_router + routing_bias
            probs = jax.nn.sigmoid(logits)
            scores, idx = jax.lax.top_k(probs, TOPK)
            scores = scores / jnp.sum(scores, axis=-1, keepdims=True)
            wts = jnp.sum(jax.nn.one_hot(idx, ER, dtype=xt.dtype) * scores[..., None], axis=1)
            g = jnp.einsum('th,ehi->tei', xt, Wg_r)
            u = jnp.einsum('th,ehi->tei', xt, Wu_r)
            hmid = silu(g) * u
            combined = jnp.einsum('tei,eih,te->th', hmid, Wd_r, wts)
            return (shared + combined).reshape(B, S, H)
        x = x + mla(rmsnorm(x, w_ln1), W_kvd, W_qd, W_ku, W_qu, W_vu, W_ropeq, W_ropek, W_o)
        x = x + moe(rmsnorm(x, w_ln2), Wg_s, Wu_s, Wd_s, Wg_r, Wu_r, Wd_r, W_router, routing_bias)
        return x
    x = L0_attn_x
    x = _layernorm(x + _L0_attn_ref(x, L0_attn_Wq, L0_attn_bq, L0_attn_Wk, L0_attn_bk, L0_attn_Wv, L0_attn_bv, L0_attn_Wo, L0_attn_bo), axis=-1)
    x = _layernorm(x + _L0_ffn_ref(x, L0_ffn_w_ln1, L0_ffn_w_ln2, L0_ffn_W_kvd, L0_ffn_W_qd, L0_ffn_W_ku, L0_ffn_W_qu, L0_ffn_W_vu, L0_ffn_W_ropeq, L0_ffn_W_ropek, L0_ffn_W_o, L0_ffn_Wg_s, L0_ffn_Wu_s, L0_ffn_Wd_s, L0_ffn_Wg_r, L0_ffn_Wu_r, L0_ffn_Wd_r, L0_ffn_W_router, L0_ffn_routing_bias), axis=-1)
    return x

_drawn_inputs = setup_inputs


def setup_inputs(seed=0):
    import zlib

    import numpy as np

    out = dict(_drawn_inputs(seed))
    spreads = {'L0_attn_bq': (0.0, 0.8),
     'L0_attn_bk': (0.0, 0.8),
     'L0_attn_bv': (0.0, 0.1),
     'L0_attn_bo': (0.0, 0.1),
     'L0_ffn_w_ln1': (1.0, 0.6),
     'L0_ffn_w_ln2': (1.0, 0.6),
     'L0_ffn_routing_bias': (0.0, 0.8)}
    factors = {'L0_attn_Wq': 8.0,
     'L0_attn_Wk': 8.0,
     'L0_ffn_W_kvd': 8.0,
     'L0_ffn_W_qd': 8.0,
     'L0_ffn_W_ku': 8.0,
     'L0_ffn_W_qu': 8.0,
     'L0_ffn_W_vu': 8.0,
     'L0_ffn_W_ropeq': 8.0,
     'L0_ffn_W_ropek': 8.0,
     'L0_ffn_W_o': 8.0,
     'L0_ffn_Wg_s': 6.137,
     'L0_ffn_Wu_s': 6.078,
     'L0_ffn_Wd_s': 6.069,
     'L0_ffn_Wg_r': 8.0,
     'L0_ffn_Wu_r': 8.0,
     'L0_ffn_Wd_r': 8.0,
     'L0_ffn_W_router': 8.0}
    for name, (base, spread) in spreads.items():
        noise = np.random.default_rng([zlib.crc32(name.encode()), seed]).standard_normal(out[name].shape)
        drawn = base * np.exp(spread * noise) if base else spread * noise
        out[name] = jnp.asarray(drawn.astype(out[name].dtype))
    for name, factor in factors.items():
        out[name] = (out[name] * factor).astype(out[name].dtype)
    return out
```

```python
from contextlib import ExitStack

import concourse.bass as bass
import concourse.mybir as mybir
import numpy as np

ALU = mybir.AluOpType
ACT = mybir.ActivationFunctionType
AX = mybir.AxisListType
F32 = mybir.dt.float32
BF16 = mybir.dt.bfloat16

P = 128
B, S, D = 4, 1024, 256
DC = D // P
ST = S // P
HALF = 512
NH = S // HALF
HEADS, HD = 16, 64
PAIRS = HEADS * HD // P
LN_EPS = 1e-5
Z_EPS = 1e-6
DMA = 16


def linear_attention(nc, x, Wq, bq, Wk, bk, Wv, bv, Wo, bo, x1, zd):
    XW = D + 1
    STEPS = PAIRS + 3
    ring_x = []
    for s in range(STEPS):
        if s < PAIRS:
            ring_x.append(("kx", s))
        if s >= 3:
            ring_x.append(("m", s - 3))
    ring_x += [("out", t) for t in range(ST)]
    X_OF = {use: i for i, use in enumerate(ring_x)}
    XN = len(ring_x)
    XP = PAIRS
    TK = ST // 2
    KN = ST * NH
    AN = TK + KN
    assert XN % 2 == 0 and AN % 2 == 0 and XP % 2 == 0

    with ExitStack() as ctx:
        def sb(name, shape, dt=F32):
            return ctx.enter_context(nc.sbuf_tensor(name, shape, dt))

        def ps(name):
            return ctx.enter_context(nc.psum_tensor(name, [P, HALF], F32))

        def sem(name):
            return ctx.enter_context(nc.semaphore(name))

        wq = sb("wq", [P, DC, HEADS * HD])
        wk = sb("wk", [P, DC, HEADS * HD])
        wv = sb("wv", [P, DC, HEADS * HD])
        wo = sb("wo", [P, PAIRS, D])
        ident = sb("ident1", [P, P])
        bq_c = sb("bq_c", [P, PAIRS])
        bq1_c = sb("bq1_c", [P, PAIRS])
        bv_c = sb("bv_c", [P, PAIRS])
        bk1 = sb("bk1", [P, HEADS * HD])
        bo_b = sb("bo_b", [P, D])
        neg1 = sb("neg1", [P, 1])
        bvwo = sb("bvwo", [P, PAIRS, D])
        xs = sb("xs", [P, ST, XW])
        xT = sb("xT", [P, DC, S])
        qf = sb("qf", [P, PAIRS, S])
        kf = sb("kf", [P, ST, HEADS * HD])
        ke, ku = sb("ke", [P, 4, HALF]), sb("ku", [P, 4, HALF])
        qe, qu = ke, ku
        kx = sb("kx", [P, PAIRS, XW])
        kxT = sb("kxT", [P, 2, DC, P])
        kvT = sb("kvT", [P, 2, P])
        mm = sb("mm", [P, PAIRS, D])
        ksb = sb("ksb", [P, PAIRS, 32])
        den = sb("den", [P, HALF // 2])
        z = sb("z", [P, HALF // 2])
        zb = sb("zb", [P, 4, S])
        bvr = zb[:, 0, :].rearrange("p (a d) -> p a d", a=PAIRS)
        res = sb("res", [P, ST, D])
        h = sb("h", [P, ST, D])
        bst = sb("bst", [P, ST, 6])
        mv = sb("mv", [P, ST, 2])
        ve, rstd, mhalf = sb("ve", [P, ST]), sb("rstd", [P, ST]), sb("mhalf", [P, ST])

        eps = sb("eps", [P, ST])

        psA = [ps(f"psA{i}") for i in range(2)]
        psQ = [ps(f"psQ{i}") for i in range(2)]
        psX = [ps(f"psX{i}") for i in range(2)]
        psT, psV = ps("psT"), ps("psV")

        w_in = sem("w_in")
        x_in = sem("x_in")
        r_in = sem("r_in")
        z_out, z_back = sem("z_out"), [sem(f"z_back{i}") for i in range(4)]
        st_done = sem("st_done")
        const_ready = sem("const_ready")
        bias_ready = sem("bias_ready")
        a_ready, a_used = sem("a_ready"), sem("a_used")
        q_ready, q_free = sem("q_ready"), sem("q_free")
        qe_free = sem("qe_free")
        x_ready, x_used = sem("x_ready"), sem("x_used")
        t_ready, kxt_ready = sem("t_ready"), sem("kxt_ready")
        v_ready, kvt_ready = sem("v_ready"), sem("kvt_ready")
        d_ready, ksb_ready = sem("d_ready"), sem("ksb_ready")
        e_ready, kf_ready = sem("e_ready"), sem("kf_ready")
        z_step, z_ready, zb_free = sem("z_step"), sem("z_ready"), sem("zb_free")
        h_free, h_step, mv_ready = sem("h_free"), sem("h_step"), sem("mv_ready")
        stats_seen = sem("stats_seen")
        rs_step, rs_ready, h_ready = sem("rs_step"), sem("rs_ready"), sem("h_ready")
        r_ready = sem("r_ready")

        block = ctx.enter_context(nc.Block())

        @block.sync
        def _(sp):
            sp.dma_start(xs[:, :, 0:D], x[0].rearrange("(s t) d -> t s d", t=P)).then_inc(x_in, DMA)
            for dst, w in ((wk, Wk), (wq, Wq), (wv, Wv)):
                sp.dma_start(dst[:], w.rearrange("(c p) h d -> p c (h d)", p=P)).then_inc(w_in, DMA)
            sp.dma_start(wo[:], Wo.rearrange("(a b) m d -> (b m) a d", b=2)).then_inc(w_in, DMA)
            for dst, v in ((bq_c, bq), (bv_c, bv)):
                sp.dma_start(dst[:], v.rearrange("(a b) m -> (b m) a", b=2),
                             allow_slow_non_contiguous=True).then_inc(w_in, DMA)
            sp.dma_start(bk1[:], bk.rearrange("h d -> (h d)").partition_broadcast(P)).then_inc(w_in, DMA)
            sp.dma_start(bo_b[:], bo.partition_broadcast(P)).then_inc(w_in, DMA)
            sp.sem_inc(h_free, 1)

            def batch(b, last):
                sp.wait_ge(x_used, b * XN + XP)
                sp.dma_start(res[:], x[b].rearrange("(s t) d -> t s d", t=P)).then_inc(r_in, DMA)
                if not last:
                    sp.wait_ge(x_ready, b * XN + (XP + X_OF[("kx", PAIRS - 1)] + 1))
                    sp.dma_start(xs[:, :, 0:D], x[b + 1].rearrange("(s t) d -> t s d", t=P)).then_inc(x_in, DMA)
                sp.wait_ge(z_ready, b + 1)
                for j in range(4):
                    sp.dma_start(zd[:, j * 256:(j + 1) * 256], z[32 * j:32 * j + HEADS, :]).then_inc(z_out, DMA)
                sp.wait_ge(z_out, b * (4 * DMA) + 4 * DMA)
                for p in range(PAIRS):
                    sp.wait_ge(zb_free, b * PAIRS + (p + 1))
                    src = zd[2 * p:2 * p + 2, :].unsqueeze(1).broadcast_to([2, HD, S])
                    sp.dma_start(zb[:, p % 4, :], src).then_inc(z_back[p % 4], DMA)
                sp.wait_ge(h_ready, b + 1)
                sp.dma_start(x1[b].rearrange("(s t) d -> t s d", t=P), h[:]).then_inc(st_done, DMA)
                sp.wait_ge(st_done, b * DMA + DMA)
                sp.sem_inc(h_free, 1)

            with sp.Fori(0, B - 1) as b:
                batch(b, False)
            batch(B - 1, True)

        @block.gpsimd
        def _(pool):
            pool.memset(ident[:], 0.0).then_inc(const_ready, 1)
            pool.memset(xs[:, :, D:XW], 1.0).then_inc(const_ready, 1)
            pool.memset(ksb[:], 0.0).then_inc(const_ready, 1)
            pool.memset(kvT[:], 0.0).then_inc(const_ready, 1)
            pool.memset(bvr, 0.0).then_inc(const_ready, 1)
            pool.memset(mhalf[:], -0.5).then_inc(const_ready, 1)
            pool.memset(eps[:], LN_EPS).then_inc(const_ready, 1)
            pool.memset(neg1[:], -1.0).then_inc(const_ready, 1)
            pool.wait_ge(const_ready, 8)
            pool.affine_select(out=ident[:], in_=ident[:], compare_op=ALU.not_equal, fill=1.0, base=0,
                               pattern=[[-1, P]], channel_multiplier=1).then_inc(const_ready, 1)
            pool.wait_ge(w_in, 8 * DMA)

            def batch(b):
                pool.wait_ge(r_in, b * DMA + DMA)
                pool.tensor_tensor(res[:], res[:], bo_b[:].unsqueeze(1).broadcast_to([P, ST, D]),
                                   ALU.add).then_inc(r_ready, 1)
                pool.wait_ge(mv_ready, b * ST + ST)
                pool.tensor_tensor(ve[:], mv[:, :, 1], eps[:], ALU.add).then_inc(rs_step, 1)
                pool.wait_ge(rs_step, b + 1)
                pool.tensor_tensor(rstd[:], ve[:], mhalf[:], ALU.pow).then_inc(rs_ready, 1)

            with pool.Fori(0, B - 1) as b:
                batch(b)
            batch(B - 1)

        @block.scalar
        def _(act):
            act.sem_inc(q_free, 2)

            def k_exp(b):
                for n in range(KN):
                    act.wait_ge(a_used, b * AN + (TK + n + 1))
                    nc.scalar.activation(ke[:, n % 4, :], ku[:, n % 4, :], ACT.Exp, bias=neg1[:]).then_inc(e_ready, 1)

            act.wait_ge(w_in, 8 * DMA)
            act.wait_ge(const_ready, 9)
            act.wait_ge(bias_ready, 4)
            k_exp(0)
            act.wait_ge(kf_ready, KN)

            def batch(b, last):
                for n in range(KN):
                    p = n // NH
                    act.wait_ge(q_ready, b * KN + (n + 1))
                    act.wait_ge(qe_free, b * KN + (n + 1))
                    nc.scalar.activation(qe[:, n % 4, :], psQ[n % 2][:], ACT.Exp, bias=bq_c[:, p:p + 1])
                    nc.scalar.activation(qu[:, n % 4, :], psQ[n % 2][:], ACT.Identity,
                                         bias=bq1_c[:, p:p + 1]).then_inc(q_free, 1)
                for s in range(STEPS):
                    if 0 <= s - 1 < PAIRS:
                        p = s - 1
                        act.wait_ge(t_ready, b * PAIRS + (p + 1))
                        nc.scalar.copy(kxT[:, p % 2, :, :].rearrange("p c d -> p (c d)"),
                                       psT[:, 0:DC * P]).then_inc(kxt_ready, 1)
                    if 0 <= s - 2 < PAIRS:
                        p = s - 2
                        act.wait_ge(v_ready, b * PAIRS + (p + 1))
                        nc.scalar.copy(kvT[0:HD, p % 2, 0:HD], psV[0:HD, 0:HD])
                        nc.scalar.copy(kvT[HD:P, p % 2, HD:P], psV[HD:P, HD:P]).then_inc(kvt_ready, 1)
                act.wait_ge(x_used, b * XN + (XP + X_OF[("kx", PAIRS - 1)] + 1))
                flat = ksb[:].rearrange("p a h -> p (a h)")
                for i in range(2):
                    rows = slice(HD * i, HD * i + HD)
                    nc.scalar.copy(flat[rows, i:i + 34 * (PAIRS - 1) + 1:34], kx[rows, :, D]).then_inc(ksb_ready, 1)
                if not last:
                    k_exp(b + 1)

            with act.Fori(0, B - 1) as b:
                batch(b, False)
            batch(B - 1, True)

        @block.vector
        def _(dve):
            dve.sem_inc(qe_free, 4)
            dve.sem_inc(zb_free, 4)
            dve.wait_ge(w_in, 8 * DMA)
            dve.wait_ge(const_ready, 9)
            dve.tensor_scalar(bq1_c[:], bq_c[:], 1.0, None, ALU.add).then_inc(bias_ready, 1)
            dve.tensor_scalar(bk1[:], bk1[:], 1.0, None, ALU.add).then_inc(bias_ready, 1)
            for i in range(2):
                rows = slice(HD * i, HD * i + HD)
                dve.tensor_copy(bvr[rows, :, HD * i:HD * i + HD],
                                bv_c[rows, :].unsqueeze(2).broadcast_to([HD, PAIRS, HD])).then_inc(bias_ready, 1)
            dve.wait_ge(bias_ready, 4)
            for p in range(PAIRS):
                dve.wait_ge(x_ready, p + 1)
                dve.tensor_copy(bvwo[:, p, :], psX[p % 2][:, 0:D]).then_inc(x_used, 1)

            def k_features(b, z_of=None):
                for n in range(TK):
                    dve.wait_ge(a_ready, b * AN + (n + 1))
                    dve.tensor_copy(xT[:, :, n * 256:(n + 1) * 256],
                                    psA[n % 2][:].rearrange("p (c t) -> p c t", c=DC)).then_inc(a_used, 1)

                if z_of is not None:
                    dve.wait_ge(qe_free, z_of * KN + (KN + 4))

                def finish(n):
                    dve.wait_ge(e_ready, b * KN + (n + 1))
                    out = kf[:, n // NH, (n % NH) * HALF:(n % NH + 1) * HALF]
                    dve.scalar_tensor_tensor(out, ke[:, n % 4, :], 1.0, ku[:, n % 4, :],
                                             ALU.min, ALU.max).then_inc(kf_ready, 1)

                for n in range(KN):
                    dve.wait_ge(a_ready, b * AN + (TK + n + 1))
                    if n >= 4 or z_of is not None:
                        dve.wait_ge(kf_ready, b * KN + (n - 3))
                    cols = slice((n % NH) * HALF, (n % NH + 1) * HALF)
                    dve.tensor_tensor(ku[:, n % 4, :], psA[(TK + n) % 2][:], bk1[:, cols], ALU.add).then_inc(a_used, 1)
                    if n >= 1:
                        finish(n - 1)
                    if z_of is not None and n >= KN - PAIRS:
                        scale_q(z_of, n - (KN - PAIRS))
                finish(KN - 1)

            def scale_q(b, p):
                dve.wait_ge(z_back[p % 4], b * (2 * DMA) + (p // 4 + 1) * DMA)
                dve.tensor_tensor(qf[:, p, :], qf[:, p, :], zb[:, p % 4, :], ALU.mult).then_inc(zb_free, 1)

            k_features(0)

            def batch(b, last):
                for n in range(KN):
                    p, half = n // NH, n % NH
                    dve.wait_ge(q_free, b * KN + (n + 3))
                    dve.scalar_tensor_tensor(qf[:, p, half * HALF:(half + 1) * HALF], qe[:, n % 4, :], 1.0,
                                             qu[:, n % 4, :], ALU.min, ALU.max).then_inc(qe_free, 1)
                for i, (what, p) in enumerate(ring_x[:2 * PAIRS]):
                    dve.wait_ge(x_ready, b * XN + (XP + i + 1))
                    if what == "kx":
                        dve.tensor_copy(kx[:, p, :], psX[i % 2][:, 0:XW]).then_inc(x_used, 1)
                    else:
                        dve.scalar_tensor_tensor(mm[:, p, :], bvwo[:, p, :], kx[:, p, D:XW], psX[i % 2][:, 0:D],
                                                 ALU.mult, ALU.add).then_inc(x_used, 1)
                dve.wait_ge(d_ready, b + 1)
                dve.tensor_scalar(den[:], psV[:, 0:HALF // 2], Z_EPS, None, ALU.add).then_inc(z_step, 1)
                dve.wait_ge(z_step, b + 1)
                dve.reciprocal(z[:], den[:]).then_inc(z_ready, 1)
                if not last:
                    k_features(b + 1, z_of=b)
                else:
                    for p in range(PAIRS):
                        scale_q(b, p)
                dve.wait_ge(r_ready, b + 1)
                dve.wait_ge(h_free, b + 1)
                for t in range(ST + 2):
                    if t < ST:
                        i = X_OF[("out", t)]
                        dve.wait_ge(x_ready, b * XN + (XP + i + 1))
                        dve.tensor_tensor(h[:, t, :], psX[i % 2][:, 0:D], res[:, t, :], ALU.add).then_inc(x_used, 1)
                    if 1 <= t <= ST:
                        dve.wait_ge(x_used, b * XN + (XP + X_OF[("out", t - 1)] + 1))
                        if t >= 2:
                            dve.wait_ge(h_step, b * ST + (t - 1))
                        dve.bn_stats(bst[:, t - 1, :], h[:, t - 1, :]).then_inc(h_step, 1)
                    if t >= 2:
                        if t == ST + 1:
                            dve.wait_ge(h_step, b * ST + ST)
                            dve.sem_inc(stats_seen, 1)
                        dve.bn_aggr(mv[:, t - 2, :], bst[:, t - 2, :]).then_inc(mv_ready, 1)
                dve.wait_ge(rs_ready, b + 1)
                for t in range(ST):
                    last_op = dve.tensor_scalar(h[:, t, :], h[:, t, :], mv[:, t, 0:1], rstd[:, t:t + 1],
                                                ALU.subtract, ALU.mult)
                last_op.then_inc(h_ready, 1)

            with dve.Fori(0, B - 1) as b:
                batch(b, False)
            batch(B - 1, True)

        @block.tensor
        def _(pe):
            pe.wait_ge(const_ready, 9)
            pe.wait_ge(w_in, 8 * DMA)
            pe.wait_ge(bias_ready, 4)
            for p in range(PAIRS):
                if p >= 2:
                    pe.wait_ge(x_used, p - 1)
                pe.matmul(psX[p % 2][:, 0:D], bvr[:, p, :], wo[:, p, :], start=True, stop=True).then_inc(x_ready, 1)

            def k_product(b, first):
                pe.wait_ge(x_in, b * DMA + DMA)
                for n in range(TK):
                    if not (first and n < 2):
                        pe.wait_ge(a_used, b * AN + (n - 1))
                    for c in range(DC):
                        for j in range(2):
                            at = (c * 2 + j) * P
                            last = pe.transpose(psA[n % 2][:, at:at + P], xs[:, 2 * n + j, c * P:(c + 1) * P], ident[:])
                    last.then_inc(a_ready, 1)
                for n in range(KN):
                    s, half = n // NH, n % NH
                    pe.wait_ge(a_used, b * AN + max(TK + n - 1, TK if n == 0 else 0))
                    for c in range(DC):
                        last = pe.matmul(psA[(TK + n) % 2][:], xT[:, c, s * P:(s + 1) * P],
                                         wk[:, c, half * HALF:(half + 1) * HALF], start=c == 0, stop=c == DC - 1)
                    last.then_inc(a_ready, 1)

            k_product(0, True)

            def batch(b, last_batch):
                for n in range(KN):
                    p, half = n // NH, n % NH
                    pe.wait_ge(q_free, b * KN + (n + 1))
                    for c in range(DC):
                        last = pe.matmul(psQ[n % 2][:], wq[:, c, p * P:(p + 1) * P],
                                         xT[:, c, half * HALF:(half + 1) * HALF], start=c == 0, stop=c == DC - 1)
                    last.then_inc(q_ready, 1)
                pe.wait_ge(kf_ready, b * KN + KN)
                for s in range(STEPS):
                    if s < PAIRS:
                        i = X_OF[("kx", s)]
                        pe.wait_ge(x_used, b * XN + (XP + i - 1))
                        for t in range(ST):
                            last = pe.matmul(psX[i % 2][:, 0:XW], kf[:, t, s * P:(s + 1) * P], xs[:, t, :],
                                             start=t == 0, stop=t == ST - 1)
                        last.then_inc(x_ready, 1)
                    if 0 <= s - 1 < PAIRS:
                        p = s - 1
                        pe.wait_ge(x_used, b * XN + (XP + X_OF[("kx", p)] + 1))
                        if p >= 1:
                            pe.wait_ge(kxt_ready, b * PAIRS + p)
                        for c in range(DC):
                            last = pe.transpose(psT[:, c * P:(c + 1) * P], kx[:, p, c * P:(c + 1) * P], ident[:])
                        last.then_inc(t_ready, 1)
                    if 0 <= s - 2 < PAIRS:
                        p = s - 2
                        pe.wait_ge(kxt_ready, b * PAIRS + (p + 1))
                        if p >= 1:
                            pe.wait_ge(kvt_ready, b * PAIRS + p)
                        for c in range(DC):
                            last = pe.matmul(psV[:, 0:P], wv[:, c, p * P:(p + 1) * P], kxT[:, p % 2, c, :],
                                             start=c == 0, stop=c == DC - 1)
                        last.then_inc(v_ready, 1)
                    if s >= 3:
                        p = s - 3
                        i = X_OF[("m", p)]
                        pe.wait_ge(kvt_ready, b * PAIRS + (p + 1))
                        pe.wait_ge(x_used, b * XN + (XP + i - 1))
                        pe.matmul(psX[i % 2][:, 0:D], kvT[:, p % 2, :], wo[:, p, :],
                                  start=True, stop=True).then_inc(x_ready, 1)
                pe.wait_ge(ksb_ready, b * 2 + 2)
                pe.wait_ge(qe_free, b * KN + (KN + 4))
                for p in range(PAIRS):
                    for j in range(4):
                        last = pe.matmul(psV[32 * j:32 * j + 32, 0:256], ksb[:, p, :], qf[:, p, j * 256:(j + 1) * 256],
                                         start=p == 0, stop=p == PAIRS - 1)
                last.then_inc(d_ready, 1)
                if not last_batch:
                    k_product(b + 1, False)
                pe.wait_ge(zb_free, b * PAIRS + (PAIRS + 4))
                pe.wait_ge(x_used, b * XN + (XP + 2 * PAIRS))
                for t in range(ST):
                    i = X_OF[("out", t)]
                    if t >= 1:
                        pe.wait_ge(x_used, b * XN + (XP + i - 1))
                    for p in range(PAIRS):
                        last = pe.matmul(psX[i % 2][:, 0:D], qf[:, p, t * P:(t + 1) * P], mm[:, p, :],
                                         start=p == 0, stop=p == PAIRS - 1)
                    last.then_inc(x_ready, 1)

            with pe.Fori(0, B - 1) as b:
                batch(b, False)
            batch(B - 1, True)



MH, MHD, ROPE_W = 16, 16, 8
LAT = 64
QK_ROWS = 96
RMS_EPS = 1e-5
VW = 32


def latent_projections(nc, x1, w_ln1, W_kvd, W_qd, W_ku, W_qu, W_vu, W_ropeq, W_ropek, rope, qp, kp, v_dram):
    K, KR, Q, QR = range(4)
    PE0, PEN = 2, 9
    LATENT, ROPEK, NOPEK, VAL0, VAL1, NOPEQ, ROPEQ, TR0, TR1 = range(9)
    PARTS = 3 * DMA

    with ExitStack() as ctx:
        def sb(name, shape, dt=F32):
            return ctx.enter_context(nc.sbuf_tensor("lp_" + name, shape, dt))

        def sem(name):
            return ctx.enter_context(nc.semaphore("lp_" + name))

        ident = sb("ident2", [P, P])
        stage = sb("stage", [P, 3, P])
        stage_r = sb("stage_r", [P, DC, P])
        w_lat = sb("w_lat", [P, DC, P])
        w_rk = sb("w_rk", [P, DC, P])
        w_up = sb("w_up", [P, 3, P])
        w_v = sb("w_v", [P, D])
        ln1 = sb("ln1", [P, DC])
        cos, sin = sb("cos", [P, S]), sb("sin", [P, S])
        xin, xn = sb("xin", [P, ST, D]), sb("xn", [P, ST, D])
        ssq, rms, rn = sb("ssq", [P, ST]), sb("rms", [P, ST]), sb("rn", [P, ST])
        inv_d, half, eps = sb("inv_d", [P, ST]), sb("half", [P, ST]), sb("eps2", [P, ST])
        xT = sb("xnT", [P, DC, S])
        lat = sb("lat", [P, S])
        rot, t1, t2 = sb("rot", [P, 2, S]), sb("t1", [P, S]), sb("t2", [P, S])
        r1 = sb("r1", [P, 4, S])
        part = sb("part", [P, 4, 3, S], BF16)
        vs = sb("vs", [P, ST, MH, VW])
        ring = [ctx.enter_context(nc.psum_tensor(f"lp_ps{i}", [P, S], F32)) for i in range(3)]

        w_in, x_in = sem("w2_in"), sem("x1_in")
        part_out = [sem(f"part_out{j}") for j in range(4)]
        v_out = sem("v_out")
        const_ready, w_ready = sem("const2_ready"), sem("w2_ready")
        pe_done, act_rel, dve_rel = sem("pe_done"), sem("act_rel"), sem("dve_rel")
        h_ready, r1_ready, m_ready, l_ready = sem("hi_ready"), sem("r1_ready"), sem("mid_ready"), sem("lo_ready")
        rope_step, rot_ready = sem("rope_step"), sem("rot_ready")
        sq_ready, rms_step, rn_step, xn_ready = sem("sq_ready"), sem("rms_step"), sem("rn_step"), sem("xn_ready")

        block = ctx.enter_context(nc.Block())

        @block.sync
        def _(sp):
            sp.dma_start(xin[:], x1[0].rearrange("(s t) d -> t s d", t=P)).then_inc(x_in, DMA)
            sp.dma_start(ln1[:], w_ln1.rearrange("(c p) -> p c", p=P), allow_slow_non_contiguous=True).then_inc(w_in, DMA)
            sp.dma_start(w_lat[:, :, 0:LAT], W_kvd.rearrange("(c p) l -> p c l", p=P)).then_inc(w_in, DMA)
            sp.dma_start(w_lat[:, :, LAT:P], W_qd.rearrange("(c p) l -> p c l", p=P)).then_inc(w_in, DMA)
            sp.dma_start(stage_r[:], W_ropek.rearrange("(c p) n -> p c n", p=P)).then_inc(w_in, DMA)
            for i, (rows, w) in enumerate(((slice(0, LAT), W_ku), (slice(LAT, P), W_qu), (slice(LAT, P), W_ropeq))):
                sp.dma_start(stage[rows, i, :], w).then_inc(w_in, DMA)
            sp.wait_ge(const_ready, 1)
            sp.dma_start(w_v[0:LAT, :], W_vu).then_inc(w_in, DMA)
            for i, table in enumerate((cos, sin)):
                sp.dma_start(table[:], rope[i].unsqueeze(1).broadcast_to([ROPE_W, MH, S])).then_inc(w_in, DMA)
            for j in range(4):
                sp.sem_inc(part_out[j], 1)
            sp.sem_inc(v_out, 1)

            def batch(b, last):
                if not last:
                    sp.wait_ge(xn_ready, b * ST + ST)
                    sp.dma_start(xin[:], x1[b + 1].rearrange("(s t) d -> t s d", t=P)).then_inc(x_in, DMA)

                def store(j):
                    dst = (kp, kp, qp, qp)[j]
                    rows = slice(P * (j % 2), P * (j % 2) + P)
                    sp.wait_ge(l_ready, b * 4 + (j + 1))
                    for i in range(3):
                        sp.dma_start(dst[b, i, rows, :], part[:, j, i, :]).then_inc(part_out[j], DMA)

                store(K)
                store(KR)
                sp.wait_ge(act_rel, b * 5 + 5)
                sp.dma_start(v_dram[b].rearrange("(s t) d -> t s d", t=P), vs[:].rearrange("p s h m -> p s (h m)")).then_inc(v_out, DMA)
                store(Q)
                store(QR)

            with sp.Fori(0, B - 1) as b:
                batch(b, False)
            batch(B - 1, True)
            for j in range(4):
                sp.wait_ge(part_out[j], B * PARTS + 1)
            sp.wait_ge(v_out, B * DMA + 1)

        @block.gpsimd
        def _(pool):
            pool.memset(w_v[:], 0.0).then_inc(const_ready, 1)
            pool.memset(w_up[:], 0.0).then_inc(const_ready, 1)
            pool.memset(ident[:], 0.0).then_inc(const_ready, 1)
            pool.memset(inv_d[:], 1.0 / D).then_inc(const_ready, 1)
            pool.memset(half[:], 0.5).then_inc(const_ready, 1)
            pool.memset(eps[:], RMS_EPS).then_inc(const_ready, 1)
            pool.memset(vs[:], 0.0).then_inc(const_ready, 1)
            pool.wait_ge(const_ready, 7)
            pool.memset(vs[:, :, :, MHD], 1.0).then_inc(const_ready, 1)
            pool.affine_select(out=ident[:], in_=ident[:], compare_op=ALU.not_equal, fill=1.0, base=0,
                               pattern=[[-1, P]], channel_multiplier=1).then_inc(const_ready, 1)

            def norm(b):
                pool.wait_ge(sq_ready, b * ST + ST)
                pool.tensor_tensor(rms[:], ssq[:], inv_d[:], ALU.mult).then_inc(rms_step, 1)
                pool.wait_ge(rms_step, b * 3 + 1)
                pool.tensor_tensor(rms[:], rms[:], half[:], ALU.pow).then_inc(rms_step, 1)
                pool.wait_ge(rms_step, b * 3 + 2)
                pool.tensor_tensor(rms[:], rms[:], eps[:], ALU.add).then_inc(rms_step, 1)

            def batch(b, last):
                for j in range(4):
                    if j == 1 and not last:
                        norm(b + 1)
                    pool.wait_ge(m_ready, b * 4 + (j + 1))
                    pool.tensor_tensor(part[:, j, 2, :], r1[:, j, :], part[:, j, 1, :], ALU.subtract).then_inc(l_ready, 1)

            norm(0)
            with pool.Fori(0, B - 1) as b:
                batch(b, False)
            batch(B - 1, True)

        @block.scalar
        def _(act):
            def squares(b):
                act.wait_ge(x_in, b * DMA + DMA)
                for s in range(ST):
                    nc.scalar.activation(xn[:, s, :], xin[:, s, :], ACT.Square, accum_out=ssq[:, s:s + 1]).then_inc(sq_ready, 1)

            def transposed(b):
                for i in range(2):
                    act.wait_ge(pe_done, b * PEN + (i + 1))
                    nc.scalar.copy(xT[:, :, i * HALF:(i + 1) * HALF],
                                   ring[(TR0 + i) % 3][:].rearrange("p (c t) -> p c t", c=DC)).then_inc(act_rel, 1)

            squares(0)
            transposed(0)
            act.wait_ge(const_ready, 9)

            def high(b, j, src):
                act.wait_ge(part_out[j], b * PARTS + 1)
                nc.scalar.copy(part[:, j, 0, :], src).then_inc(h_ready, 1)

            def batch(b, last):
                act.wait_ge(pe_done, b * PEN + (PE0 + LATENT + 1))
                nc.scalar.copy(lat[:], ring[LATENT % 3][:]).then_inc(act_rel, 1)
                act.wait_ge(pe_done, b * PEN + (PE0 + NOPEK + 1))
                high(b, K, ring[NOPEK % 3][:])
                act.wait_ge(rot_ready, b * 2 + 1)
                high(b, KR, rot[:, 0, :])
                act.wait_ge(v_out, b * DMA + 1)
                for i in range(2):
                    act.wait_ge(pe_done, b * PEN + (PE0 + VAL0 + i + 1))
                    nc.scalar.copy(vs[:, 4 * i:4 * i + 4, :, 0:MHD].rearrange("p s h m -> p (s h) m"),
                                   ring[(VAL0 + i) % 3][:].rearrange("p (a m) -> p a m", m=MHD)).then_inc(act_rel, 1)
                if not last:
                    act.wait_ge(rms_step, b * 3 + 3)
                    squares(b + 1)
                act.wait_ge(pe_done, b * PEN + (PE0 + NOPEQ + 1))
                high(b, Q, ring[NOPEQ % 3][:])
                act.wait_ge(rot_ready, b * 2 + 2)
                high(b, QR, rot[:, 1, :])
                if not last:
                    transposed(b + 1)

            with act.Fori(0, B - 1) as b:
                batch(b, False)
            batch(B - 1, True)

        @block.vector
        def _(dve):
            dve.sem_inc(dve_rel, 1)
            dve.wait_ge(w_in, 10 * DMA)
            dve.wait_ge(const_ready, 9)
            def by_feature(w):
                return w.rearrange("p (h d) -> p d h", h=MH)
            def columns(w):
                return w.rearrange("p (d h) -> p d h", h=MH)
            for c in range(DC):
                dve.tensor_scalar(columns(w_rk[:, c, :]), by_feature(stage_r[:, c, :]), ln1[:, c:c + 1], None,
                                  ALU.mult).then_inc(w_ready, 1)
                dve.tensor_scalar(w_lat[:, c, :], w_lat[:, c, :], ln1[:, c:c + 1], None, ALU.mult).then_inc(w_ready, 1)
            for i, rows in enumerate((slice(0, LAT), slice(LAT, P), slice(LAT, P))):
                scale = 1.0 if i == 0 else float(MHD) ** -0.5
                dve.tensor_scalar(columns(w_up[rows, i, :]), by_feature(stage[rows, i, :]), scale, None,
                                  ALU.mult).then_inc(w_ready, 1)

            def normalise(b):
                dve.wait_ge(rms_step, b * 3 + 3)
                dve.reciprocal(rn[:], rms[:]).then_inc(rn_step, 1)
                dve.wait_ge(rn_step, b + 1)
                if not (isinstance(b, int) and b == 0):
                    dve.wait_ge(pe_done, (b - 1) * PEN + PE0)
                for s in range(ST):
                    dve.tensor_scalar(xn[:, s, :], xin[:, s, :], rn[:, s:s + 1], None, ALU.mult).then_inc(xn_ready, 1)

            normalise(0)

            def rotate(b, i, use):
                src = ring[use % 3]
                dve.wait_ge(pe_done, b * PEN + (PE0 + use + 1))
                dve.tensor_tensor(t1[:], src[:], cos[:], ALU.mult).then_inc(rope_step, 1)
                dve.tensor_tensor(t2[0:64, :], src[64:P, :], sin[0:64, :], ALU.mult)
                dve.tensor_tensor(t2[64:P, :], src[0:64, :], sin[64:P, :], ALU.mult).then_inc(dve_rel, 1)
                dve.wait_ge(rope_step, b * 2 + (i + 1))
                dve.wait_ge(dve_rel, b * 4 + (2 if i == 0 else 5))
                dve.tensor_tensor(rot[:, i, :], t1[:], t2[:], ALU.add).then_inc(rot_ready, 1)

            def split(b, j, src, rel):
                dve.wait_ge(h_ready, b * 4 + (j + 1))
                dve.wait_ge(part_out[j], b * PARTS + 1)
                dve.tensor_tensor(r1[:, j, :], src, part[:, j, 0, :], ALU.subtract).then_inc(rel, 1)

            def middle(b, j):
                dve.tensor_copy(part[:, j, 1, :], r1[:, j, :]).then_inc(m_ready, 1)

            def batch(b, last):
                rotate(b, 0, ROPEK)
                split(b, K, ring[NOPEK % 3][:], dve_rel)
                dve.wait_ge(dve_rel, b * 4 + 3)
                middle(b, K)
                split(b, KR, rot[:, 0, :], r1_ready)
                dve.wait_ge(r1_ready, b * 2 + 1)
                middle(b, KR)
                if not last:
                    normalise(b + 1)
                split(b, Q, ring[NOPEQ % 3][:], dve_rel)
                dve.wait_ge(dve_rel, b * 4 + 4)
                middle(b, Q)
                rotate(b, 1, ROPEQ)
                split(b, QR, rot[:, 1, :], r1_ready)
                dve.wait_ge(r1_ready, b * 2 + 2)
                middle(b, QR)

            with dve.Fori(0, B - 1) as b:
                batch(b, False)
            batch(B - 1, True)

        @block.tensor
        def _(pe):
            pe.wait_ge(const_ready, 9)

            def transposes(b, first):
                pe.wait_ge(xn_ready, b * ST + ST)
                for i in range(2):
                    if not first:
                        if i == 0:
                            pe.wait_ge(act_rel, (b - 1) * 5 + 5)
                        else:
                            pe.wait_ge(dve_rel, (b - 1) * 4 + 4)
                    for c in range(DC):
                        for s in range(4):
                            at = c * HALF + s * P
                            last = pe.transpose(ring[(TR0 + i) % 3][:, at:at + P], xn[:, 4 * i + s, c * P:(c + 1) * P], ident[:])
                    last.then_inc(pe_done, 1)

            transposes(0, True)
            pe.wait_ge(w_ready, 7)

            def project(use, pairs):
                for h in range(NH):
                    cols = slice(h * HALF, (h + 1) * HALF)
                    for i, (w, src) in enumerate(pairs):
                        last = pe.matmul(ring[use % 3][:, cols], w, src[:, cols], start=i == 0, stop=i == len(pairs) - 1)
                last.then_inc(pe_done, 1)

            def batch(b, last_batch):
                pe.wait_ge(act_rel, b * 5 + 2)
                pe.wait_ge(dve_rel, b * 4 + 1)
                project(LATENT, [(w_lat[:, c, :], xT[:, c, :]) for c in range(DC)])
                project(ROPEK, [(w_rk[:, c, :], xT[:, c, :]) for c in range(DC)])
                pe.wait_ge(act_rel, b * 5 + 3)
                project(NOPEK, [(w_up[:, 0, :], lat[:])])
                for i in range(2):
                    if i == 1:
                        pe.wait_ge(dve_rel, b * 4 + 2)
                    for s in range(4):
                        at = (4 * i + s) * P
                        last = pe.matmul(ring[(VAL0 + i) % 3][:, s * D:(s + 1) * D], lat[:, at:at + P], w_v[:],
                                         start=s % 2 == 0, stop=s % 2 == 1, skip_group_check=True)
                    last.then_inc(pe_done, 1)
                pe.wait_ge(dve_rel, b * 4 + 3)
                project(NOPEQ, [(w_up[:, 1, :], lat[:])])
                pe.wait_ge(act_rel, b * 5 + 4)
                project(ROPEQ, [(w_up[:, 2, :], lat[:])])
                if not last_batch:
                    transposes(b + 1, False)

            with pe.Fori(0, B - 1) as b:
                batch(b, False)
            batch(B - 1, True)


def rope_table():
    import numpy as np
    inv = (1.0 / np.float32(10000.0) ** (np.arange(0, ROPE_W, 2, dtype=np.float32) / np.float32(ROPE_W))).astype(np.float32)
    angle = np.arange(S, dtype=np.float32)[None, :] * np.concatenate([inv, inv])[:, None]
    sign = np.where(np.arange(ROPE_W) < ROPE_W // 2, -1, 1).astype(np.float32)[:, None]
    return np.stack([np.cos(angle), np.sin(angle) * sign]).astype(np.float32)



GH = 4
NG = MH // GH
HI, MID, LO = range(3)
ROWS = QK_ROWS + 3
NEG = -3.0e38
Y_UNITS = [(i, jj, part) for i in range(ST) for part in range(i // 4 + 1) for jj in range(GH // 2)]
Y_STEPS = [(0, i) for i in range(4)] + [(1, i) for i in range(ST)]


def softmax_attention(nc, qp, kp, v_dram, y_dram):
    UN, SN = len(Y_UNITS), len(Y_STEPS)
    EN = SN * GH
    LOAD = 7 * DMA

    def at(b, g, per, n):
        return b * (NG * per) + (g * per + n)

    with ExitStack() as ctx:
        def sb(name, shape, dt=F32):
            return ctx.enter_context(nc.sbuf_tensor("sm_" + name, shape, dt))

        def sem(name):
            return ctx.enter_context(nc.semaphore("sm_" + name))

        qs = [sb(f"qs{i}", [ROWS, GH, S], BF16) for i in range(NG)]
        ks = [sb(f"ks{i}", [ROWS, GH, S], BF16) for i in range(NG)]
        vp = [sb(f"vp{i}", [P, ST, GH * VW]) for i in range(NG)]
        pt = [sb(f"pt{i}", [P, GH, HALF]) for i in range(3)]
        ident = sb("ident3", [P, P], BF16)
        mask = sb("mask", [P, P], BF16)
        mask_t = sb("mask_t", [P, P], BF16)
        zero = sb("zero", [P, GH * ST])
        mx = [sb(f"mx{i}", [P, 2, ST, GH]) for i in range(2)]
        neg = [sb(f"neg{i}", [P, GH * ST]) for i in range(2)]
        rem = [sb(f"rem{i}", [P, GH * ST]) for i in range(2)]
        nb = [sb(f"nb{i}", [P, 3, GH * ST], BF16) for i in range(2)]
        mt = [sb(f"mt{i}", [QK_ROWS, P], BF16) for i in range(2)]
        yb = [sb(f"yb{i}", [P, HALF]) for i in range(2)]
        psA = [ctx.enter_context(nc.psum_tensor(f"sm_psMax{i}", [P, 2, HALF], F32)) for i in range(2)]
        psB = [ctx.enter_context(nc.psum_tensor(f"sm_psS{i}", [P, HALF], F32)) for i in range(2)]
        psO = ctx.enter_context(nc.psum_tensor("psO", [P, HALF], F32))
        psM = ctx.enter_context(nc.psum_tensor("psM", [P, 2 * HALF], BF16))

        load_in = [sem(f"load_in{i}") for i in range(NG)]
        m_in = sem("m_in")
        y_out = [sem(f"y_out{i}") for i in range(2)]
        const_ready = sem("const3_ready")
        max_ready, max_used = sem("max_ready"), sem("max_used")
        mx_ready, neg_step = sem("mx_ready"), sem("neg_step")
        mt_ready, mt_copied = sem("mt_ready"), sem("mt_copied")
        s_ready, e_ready = sem("s_ready"), sem("exp_ready")
        y_turn = sem("y_turn")
        pv_done, y_copied = sem("pv_done"), sem("y_copied")

        block = ctx.enter_context(nc.Block())

        @block.sync
        def _(sp):
            for i in range(2):
                sp.sem_inc(y_out[i], 1)

            def load(b, g):
                b, g = (b, g) if g < NG else (b + 1, g - NG)

                def rows(src, part, n, same):
                    f = src[b, part].rearrange("(d h) t -> d h t", h=MH)[:, GH * g:GH * g + GH, :]
                    if n == 1:
                        return f.rearrange("d h t -> d (h t)")
                    if same:
                        return f.rearrange("d h t -> d (h t)").unsqueeze(0).broadcast_to([n, MHD, GH * S])
                    return src[b, part:part + n].rearrange("c (d h) t -> c d h t", h=MH)[:, :, GH * g:GH * g + GH, :]\
                        .rearrange("c d h t -> c d (h t)")

                for dst, src, same in ((qs[g], qp, True), (ks[g], kp, False)):
                    for lo, n, part in ((0, 3, HI), (48, 2, MID if same else HI), (80, 1, LO if same else HI)):
                        sp.dma_start(dst[lo:lo + 16 * n].rearrange("p h t -> p (h t)"),
                                     rows(src, part, n, same)).then_inc(load_in[g], DMA)
                sp.dma_start(vp[g][:], v_dram[b].rearrange("(i t) c -> t i c", t=P)[
                    :, :, g * GH * VW:(g + 1) * GH * VW]).then_inc(load_in[g], DMA)

            def store_maxima(b, g):
                sp.wait_ge(mt_copied, at(b, g, 1, 2))
                dst, src = qs[(g + 1) % NG], mt[(g + 1) % 2]
                for part in range(3):
                    sp.dma_start(dst[QK_ROWS + part:QK_ROWS + part + 1].rearrange("p h (i t) -> p (h i) t", t=P),
                                 src[part * 32:(part + 1) * 32, :]).then_inc(m_in, DMA)

            def store_y(b, g, qh):
                sp.wait_ge(y_copied, at(b, g, 2, qh + 1))
                sp.sem_inc(y_turn, 1)
                sp.dma_start(y_dram[b, qh, g], yb[qh][:]).then_inc(y_out[qh], DMA)

            sp.wait_ge(const_ready, 11)
            for g in range(3):
                load(0, g)
            store_maxima(0, -1)

            def group(b, g, last):
                if not (last and g == NG - 1):
                    sp.wait_ge(pv_done, at(b, g, SN, 3))
                if not (last and g > 0):
                    load(b, g + 3)
                store_y(b, g, 0)
                if not (last and g == NG - 1):
                    store_maxima(b, g)
                store_y(b, g, 1)

            with sp.Fori(0, B - 1) as b:
                for g in range(NG):
                    group(b, g, False)
            for g in range(NG):
                group(B - 1, g, True)
            for i in range(2):
                sp.wait_ge(y_out[i], B * NG * DMA + 1)

        @block.gpsimd
        def _(pool):
            pool.memset(zero[:], 0.0).then_inc(const_ready, 1)
            pool.memset(ident[:], 0.0).then_inc(const_ready, 1)
            pool.memset(mask[:], 0.0).then_inc(const_ready, 1)
            pool.memset(mask_t[:], 0.0).then_inc(const_ready, 1)
            pool.wait_ge(const_ready, 4 + NG)
            pool.affine_select(out=ident[:], in_=ident[:], compare_op=ALU.not_equal, fill=1.0, base=0,
                               pattern=[[-1, P]], channel_multiplier=1).then_inc(const_ready, 1)
            pool.affine_select(out=mask[:], in_=mask[:], compare_op=ALU.is_ge, fill=NEG, base=0,
                               pattern=[[-1, P]], channel_multiplier=1).then_inc(const_ready, 1)
            pool.affine_select(out=mask_t[:], in_=mask_t[:], compare_op=ALU.is_ge, fill=NEG, base=0,
                               pattern=[[1, P]], channel_multiplier=-1).then_inc(const_ready, 1)

            def negate(b, g, par):
                def done(n):
                    return at(b, g, 5, n)
                pool.wait_ge(mx_ready, at(b, g, 1, 1))
                pool.tensor_tensor(neg[par][:].rearrange("p (j i) -> p j i", j=GH), zero[:].rearrange("p (j i) -> p j i", j=GH),
                                   mx[par][:, 0].rearrange("p i j -> p j i"), ALU.subtract).then_inc(neg_step, 1)
                pool.wait_ge(neg_step, done(1))
                pool.tensor_tensor(nb[par][:, HI], neg[par][:], zero[:], ALU.add).then_inc(neg_step, 1)
                pool.wait_ge(neg_step, done(2))
                pool.tensor_tensor(rem[par][:], neg[par][:], nb[par][:, HI], ALU.subtract).then_inc(neg_step, 1)
                pool.wait_ge(neg_step, done(3))
                pool.tensor_tensor(nb[par][:, MID], rem[par][:], zero[:], ALU.add).then_inc(neg_step, 1)
                pool.wait_ge(neg_step, done(4))
                pool.tensor_tensor(nb[par][:, LO], rem[par][:], nb[par][:, MID], ALU.subtract).then_inc(neg_step, 1)

            negate(0, 0, 0)

            def group(b, g, last):
                if not (last and g == NG - 1):
                    negate(b, g + 1, (g + 1) % 2)

            with pool.Fori(0, B - 1) as b:
                for g in range(NG):
                    group(b, g, False)
            for g in range(NG):
                group(B - 1, g, True)

        @block.vector
        def _(dve):
            dve.sem_inc(max_used, 2)
            for i in range(NG):
                dve.memset(ks[i][QK_ROWS:ROWS], 1.0).then_inc(const_ready, 1)

            def unit(b, g, u):
                g, par = g, g % 2
                i, jj, part = Y_UNITS[u]
                if u == 0 and not (isinstance(b, int) and b == 0 and g < 2):
                    dve.wait_ge(neg_step, at(b, g - 2, 5, 1))
                w = P * (i + 1) - HALF * part if part == i // 4 else HALF
                dve.wait_ge(max_ready, at(b, g, UN, u + 1))
                dve.tensor_reduce(mx[par][:, part, i, 2 * jj:2 * jj + 2], psA[u % 2][:, :, 0:w],
                                  AX.X, ALU.max).then_inc(max_used, 1)
                if u == UN - 1:
                    dve.wait_ge(max_used, at(b, g, UN, UN + 2))
                    dve.tensor_tensor(mx[par][:, 0, 4:ST], mx[par][:, 0, 4:ST], mx[par][:, 1, 4:ST],
                                      ALU.max).then_inc(mx_ready, 1)

            for u in range(UN):
                unit(0, 0, u)
            for u in range(UN // 2):
                unit(0, 1, u)

            def group(b, g, last):
                for k in range(SN):
                    ahead, us = (1, (12 + 2 * k, 13 + 2 * k)) if k < 6 else (2, (2 * k - 12, 2 * k - 11))
                    if not (last and g + ahead >= NG):
                        for u in us:
                            unit(b, g + ahead, u)

            with dve.Fori(0, B - 1) as b:
                for g in range(NG):
                    group(b, g, False)
            for g in range(NG):
                group(B - 1, g, True)

        @block.scalar
        def _(act):
            act.sem_inc(e_ready, 2)

            def copy_maxima(b, g):
                par = (g + 1) % 2
                act.wait_ge(mt_ready, at(b, g, 1, 2))
                nc.scalar.copy(mt[par][:], psM[0:QK_ROWS, 0:P]).then_inc(mt_copied, 1)

            def copy_y(b, g, qh):
                act.wait_ge(pv_done, at(b, g, SN, (SN if qh else 4) + 3))
                act.wait_ge(y_out[qh], at(b, g, DMA, 1))
                nc.scalar.copy(yb[qh][:], psO[:]).then_inc(y_copied, 1)

            copy_maxima(0, -1)

            def group(b, g, first, last):
                for k, (qh, i) in enumerate(Y_STEPS):
                    q0 = max(HALF * qh, P * i)
                    n = HALF * (qh + 1) - q0
                    for j in range(GH):
                        act.wait_ge(s_ready, at(b, g, EN, k * GH + j + 1))
                        if j == 0:
                            act.wait_ge(pv_done, at(b, g, SN, k + 1))
                        nc.scalar.activation(pt[k % 3][:, j, 0:n], psB[j % 2][:, 0:n], ACT.Exp).then_inc(e_ready, 1)
                        if j == 1 and k == 1 and not (first and g == 0):
                            copy_y(b, g - 1, 1)
                        if j == 1 and k == 5:
                            copy_y(b, g, 0)
                        if j == 1 and k == 9 and not (last and g == NG - 1):
                            copy_maxima(b, g)

            for g in range(NG):
                group(0, g, True, False)
            with act.Fori(1, B - 1) as b:
                for g in range(NG):
                    group(b, g, False, False)
            for g in range(NG):
                group(B - 1, g, False, True)
            copy_y(B - 1, NG - 1, 1)

        @block.tensor
        def _(pe):
            pe.sem_inc(pv_done, 3)
            pe.wait_ge(const_ready, 11)

            def unit(b, g, u):
                i, jj, part = Y_UNITS[u]
                if u == 0:
                    over = g // NG
                    pe.wait_ge(load_in[g % NG], (b + over) * LOAD + LOAD)
                diagonal = part == i // 4
                w = P * (i + 1) - HALF * part if diagonal else HALF
                q, kk = qs[g % NG], ks[g % NG]
                pe.wait_ge(max_used, at(b, g, UN, u + 1))
                for a in range(2):
                    j = 2 * jj + a
                    last = pe.matmul(psA[u % 2][:, a, 0:w], q[0:QK_ROWS, j, i * P:(i + 1) * P],
                                     kk[0:QK_ROWS, j, part * HALF:part * HALF + w], start=True, stop=not diagonal)
                    if diagonal:
                        last = pe.matmul(psA[u % 2][:, a, w - P:w], ident[:], mask[:], start=False, stop=True)
                last.then_inc(max_ready, 1)

            def transpose_maxima(b, g):
                par = (g + 1) % 2
                pe.wait_ge(neg_step, at(b, g, 5, 10))
                if not (isinstance(b, int) and b == 0 and g == -1):
                    pe.wait_ge(mt_copied, at(b, g, 1, 1))
                pe.transpose(psM[0:QK_ROWS, 0:P], nb[par][:].rearrange("p c n -> p (c n)"), ident[:]).then_inc(mt_ready, 1)

            for u in range(UN):
                unit(0, 0, u)
            for u in range(UN // 2):
                unit(0, 1, u)
            transpose_maxima(0, -1)

            def weighted_sum(b, g, k):
                qh, i = Y_STEPS[k]
                q0 = max(HALF * qh, P * i)
                n = HALF * (qh + 1) - q0
                pe.wait_ge(e_ready, at(b, g, EN, (k + 1) * GH + 2))
                if i == 0 and not (isinstance(b, int) and b == 0 and g == 0 and qh == 0):
                    pe.wait_ge(y_copied, at(b, g, 2, qh))
                for j in range(GH):
                    last = pe.matmul(psO[VW * j:VW * (j + 1), q0 - HALF * qh:HALF], vp[g % NG][:, i, VW * j:VW * (j + 1)],
                                     pt[k % 3][:, j, 0:n], start=i == 0, stop=i == 4 * qh + 3)
                last.then_inc(pv_done, 1)

            def group(b, g, first, last):
                for k, (qh, i) in enumerate(Y_STEPS):
                    q0 = max(HALF * qh, P * i)
                    n = HALF * (qh + 1) - q0
                    if k == 0:
                        pe.wait_ge(m_in, at(b, g, 3 * DMA, 3 * DMA))
                    ahead, us = (1, (12 + 2 * k, 13 + 2 * k)) if k < 6 else (2, (2 * k - 12, 2 * k - 11))
                    for j in range(GH):
                        pe.wait_ge(e_ready, at(b, g, EN, k * GH + j + 1))
                        diagonal = i // 4 == qh
                        done = pe.matmul(psB[j % 2][:, 0:n], ks[g][:, j, i * P:(i + 1) * P], qs[g][:, j, q0:q0 + n],
                                         start=True, stop=not diagonal)
                        if diagonal:
                            done = pe.matmul(psB[j % 2][:, 0:P], ident[:], mask_t[:], start=False, stop=True)
                        done.then_inc(s_ready, 1)
                        if j % 2 == 1 and not (last and g + ahead >= NG):
                            unit(b, g + ahead, us[j // 2])
                    if k == 9 - 1 and not (last and g == NG - 1):
                        transpose_maxima(b, g)
                    if k >= 1:
                        weighted_sum(b, g, k - 1)
                    elif not (first and g == 0):
                        weighted_sum(b if g > 0 else b - 1, g - 1 if g > 0 else NG - 1, SN - 1)

            for g in range(NG):
                group(0, g, True, False)
            with pe.Fori(1, B - 1) as b:
                for g in range(NG):
                    group(b, g, False, False)
            for g in range(NG):
                group(B - 1, g, False, True)
            weighted_sum(B - 1, NG - 1, SN - 1)



NBLK = B * NH
TT = HALF // P
ER = 7
NE = ER + 1


def output_and_router(nc, y_dram, x1, W_o, w_ln2, W_router, routing_bias, x12, xT2, wts):
    with ExitStack() as ctx:
        def sb(name, shape, dt=F32):
            return ctx.enter_context(nc.sbuf_tensor("rt_" + name, shape, dt))

        def ps(name):
            return ctx.enter_context(nc.psum_tensor("rt_" + name, [P, HALF], F32))

        def sem(name):
            return ctx.enter_context(nc.semaphore("rt_" + name))

        ident = sb("ident4", [P, P])
        wo = sb("wo4", [P, DC, D])
        wr = sb("wr", [P, DC, ER])
        ln2 = sb("ln2", [P, DC])
        rb = sb("rb", [P, ER])
        rank = sb("rank", [P, NBLK * TT, ER])
        half, inv_d, eps = sb("half4", [P, TT]), sb("inv_d4", [P, TT]), sb("eps4", [P, TT])
        yT = sb("yT", [P, NG, HALF])
        x1b = sb("x1b", [P, TT, D])
        rden = sb("rden", [P, TT, MH])
        yn = sb("yn", [P, TT, D])
        ynT = sb("ynT", [P, DC, HALF])
        x2s, xn = sb("x2s", [P, TT, D]), sb("xn4", [P, TT, D])
        ssq, rms, rn = sb("ssq4", [P, TT]), sb("rms4", [P, TT]), sb("rn4", [P, TT])
        xnT = sb("xnT4", [P, DC, HALF])
        logit = sb("logit", [P, NBLK * TT, ER])
        prob, tie, hot1, hot2 = (sb(n, [P, NBLK * TT, ER]) for n in ("prob", "tie", "hot1", "hot2"))
        top1, top2, pick, total = (sb(n, [P, NBLK * TT]) for n in ("top1", "top2", "pick", "total"))
        psY, psT, psW = ([ps(f"{n}{i}") for i in range(2)] for n in ("psY", "psT4", "psW"))
        psL = ps("psL")

        w_in, y_in, x1_in = sem("w4_in"), sem("y_in"), sem("x1b_in")
        x12_out, xT_out = sem("x12_out"), sem("xT_out")
        const_ready, w_ready = sem("const4_ready"), sem("w4_ready")
        y_ready, y_used, t_ready, t_used = sem("yT_ready"), sem("yT_used"), sem("t4_ready"), sem("t4_used")
        den_ready = sem("den_ready")
        o_ready, x2_ready, sq_ready = sem("o4_ready"), sem("x2_ready"), sem("sq4_ready")
        rms_step, rn_ready, xn_ready = sem("rms4_step"), sem("rn4_ready"), sem("xn4_ready")
        sum_ready = sem("sum_ready")
        l_ready, l_used, chain = sem("l4_ready"), sem("l4_used"), sem("router_step")
        p_ready, turn = sem("prob_ready"), sem("turn4")

        block = ctx.enter_context(nc.Block())

        def rows(t_dram, t):
            return t_dram.rearrange("b (h s p) d -> (b h) p s d", h=NH, p=P)[t]

        @block.sync
        def _(sp):
            sp.dma_start(yT[:], y_dram.rearrange("b h g p t -> (b h) p g t")[0]).then_inc(y_in, DMA)
            sp.dma_start(x1b[:], rows(x1, 0)).then_inc(x1_in, DMA)
            sp.dma_start(wo[:], W_o.rearrange("(c p) n -> p c n", p=P)).then_inc(w_in, DMA)
            sp.dma_start(wr[:], W_router.rearrange("(c p) n -> p c n", p=P)).then_inc(w_in, DMA)
            sp.dma_start(ln2[:], w_ln2.rearrange("(c p) -> p c", p=P), allow_slow_non_contiguous=True).then_inc(w_in, DMA)
            sp.dma_start(rb[:], routing_bias.partition_broadcast(P)).then_inc(w_in, DMA)
            sp.sem_inc(x12_out, 1)
            sp.sem_inc(xT_out, 1)

            def body(t, last):
                if not last:
                    sp.wait_ge(y_ready, t * TT + TT)
                    sp.sem_inc(turn, 1)
                    sp.dma_start(yT[:], y_dram.rearrange("b h g p t -> (b h) p g t")[t + 1]).then_inc(y_in, DMA)
                    sp.wait_ge(sum_ready, t + 1)
                    sp.sem_inc(turn, 1)
                    sp.dma_start(x1b[:], rows(x1, t + 1)).then_inc(x1_in, DMA)
                sp.wait_ge(sum_ready, t + 1)
                sp.sem_inc(turn, 1)
                sp.dma_start(rows(x12, t), x2s[:]).then_inc(x12_out, DMA)
                sp.wait_ge(t_used, t * 4 + 4)
                sp.sem_inc(turn, 1)
                sp.dma_start(xT2[t], xnT[:]).then_inc(xT_out, DMA)

            with sp.Fori(0, NBLK - 1) as t:
                body(t, False)
            body(NBLK - 1, True)
            sp.wait_ge(x12_out, NBLK * DMA + 1)
            sp.wait_ge(xT_out, NBLK * DMA + 1)

        @block.gpsimd
        def _(pool):
            pool.memset(ident[:], 0.0).then_inc(const_ready, 1)
            pool.memset(half[:], 0.5).then_inc(const_ready, 1)
            pool.memset(inv_d[:], 1.0 / D).then_inc(const_ready, 1)
            pool.memset(eps[:], RMS_EPS).then_inc(const_ready, 1)
            pool.memset(wts[:, :, 0], 1.0).then_inc(const_ready, 1)
            for e in range(ER):
                pool.memset(rank[:, :, e], float(ER - e)).then_inc(const_ready, 1)
            pool.wait_ge(const_ready, 5 + ER)
            pool.affine_select(out=ident[:], in_=ident[:], compare_op=ALU.not_equal, fill=1.0, base=0,
                               pattern=[[-1, P]], channel_multiplier=1).then_inc(const_ready, 1)
            with pool.Fori(0, NBLK) as t:
                pool.wait_ge(sq_ready, t * TT + TT)
                pool.tensor_tensor(rms[:], ssq[:], inv_d[:], ALU.mult).then_inc(rms_step, 1)
                pool.wait_ge(rms_step, t * 3 + 1)
                pool.tensor_tensor(rms[:], rms[:], half[:], ALU.pow).then_inc(rms_step, 1)
                pool.wait_ge(rms_step, t * 3 + 2)
                pool.tensor_tensor(rms[:], rms[:], eps[:], ALU.add).then_inc(rms_step, 1)

        @block.scalar
        def _(act):
            def first(t):
                for i in range(2):
                    act.wait_ge(t_ready, t * 4 + (i + 1))
                    nc.scalar.copy(ynT[:, :, i * 256:(i + 1) * 256], psT[i][:].rearrange("p (c n) -> p c n", c=DC)).then_inc(t_used, 1)

            def second(t):
                for s in range(TT):
                    act.wait_ge(x2_ready, t * TT + (s + 1))
                    nc.scalar.activation(xn[:, s, :], x2s[:, s, :], ACT.Square, accum_out=ssq[:, s:s + 1]).then_inc(sq_ready, 1)
                act.wait_ge(xT_out, t * DMA + 1)
                for i in range(2):
                    act.wait_ge(t_ready, t * 4 + (i + 3))
                    nc.scalar.copy(xnT[:, :, i * 256:(i + 1) * 256], psT[i][:].rearrange("p (c n) -> p c n", c=DC)).then_inc(t_used, 1)

            with act.Fori(0, NBLK) as t:
                first(t)
                second(t)
            act.wait_ge(l_used, NBLK)
            nc.scalar.activation(prob[:], logit[:], ACT.Sigmoid).then_inc(p_ready, 1)

        @block.vector
        def _(dve):
            dve.wait_ge(w_in, 4 * DMA)
            dve.wait_ge(const_ready, 6 + ER)
            for c in range(DC):
                dve.tensor_scalar(wr[:, c, :], wr[:, c, :], ln2[:, c:c + 1], None, ALU.mult).then_inc(w_ready, 1)

            def first(t):
                for s in range(TT):
                    src = psY[s % 2][:].rearrange("p (h m) -> p h m", m=VW)
                    dve.wait_ge(y_ready, t * TT + (s + 1))
                    dve.reciprocal(rden[:, s, :], src[:, :, MHD]).then_inc(den_ready, 1)
                    dve.wait_ge(den_ready, t * TT + (s + 1))
                    dve.tensor_tensor(yn[:, s, :].rearrange("p (h m) -> p h m", m=MHD), src[:, :, 0:MHD],
                                      rden[:, s, :].unsqueeze(2).broadcast_to([P, MH, MHD]), ALU.mult).then_inc(y_used, 1)

            def second(t):
                dve.wait_ge(x1_in, t * DMA + DMA)
                dve.wait_ge(x12_out, t * DMA + 1)
                for s in range(TT):
                    dve.wait_ge(o_ready, t * 2 + (s // 2 + 1))
                    dve.tensor_tensor(x2s[:, s, :], psW[s // 2][:, (s % 2) * D:(s % 2 + 1) * D], x1b[:, s, :],
                                      ALU.add).then_inc(x2_ready, 1)
                dve.wait_ge(rms_step, t * 3 + 3)
                dve.reciprocal(rn[:], rms[:]).then_inc(rn_ready, 1)
                dve.wait_ge(rn_ready, t + 1)
                for s in range(TT):
                    dve.tensor_scalar(xn[:, s, :], x2s[:, s, :], rn[:, s:s + 1], None, ALU.mult).then_inc(xn_ready, 1)
                dve.wait_ge(xn_ready, t * TT + TT)
                dve.tensor_tensor(x2s[:], x2s[:], x1b[:], ALU.add).then_inc(sum_ready, 1)

            def logits(t):
                dve.wait_ge(l_ready, t + 1)
                dve.tensor_tensor(logit[:, bass.ts(t, TT), :], psL[:, 0:8 * TT].rearrange("p (s e) -> p s e", e=8)[:, :, 0:ER],
                                  rb[:].unsqueeze(1).broadcast_to([P, TT, ER]), ALU.add).then_inc(l_used, 1)

            with dve.Fori(0, NBLK) as t:
                first(t)
                second(t)
                logits(t)

            steps = [0]

            def then(ins):
                steps[0] += 1
                ins.then_inc(chain, 1)
                dve.wait_ge(chain, steps[0])

            def wide(v):
                return v[:].unsqueeze(2).broadcast_to([P, NBLK * TT, ER])

            dve.wait_ge(p_ready, 1)
            for top, hot in ((top1, hot1), (top2, hot2)):
                then(dve.tensor_reduce(top[:], prob[:], AX.X, ALU.max))
                then(dve.tensor_tensor(tie[:], prob[:], wide(top), ALU.is_equal))
                then(dve.tensor_tensor(tie[:], tie[:], rank[:], ALU.mult))
                then(dve.tensor_reduce(pick[:], tie[:], AX.X, ALU.max))
                then(dve.tensor_tensor(hot[:], tie[:], wide(pick), ALU.is_equal))
                if hot is hot1:
                    then(dve.scalar_tensor_tensor(prob[:], hot[:], -2.0, prob[:], ALU.mult, ALU.add))
            then(dve.tensor_tensor(total[:], top1[:], top2[:], ALU.add))
            then(dve.reciprocal(total[:], total[:]))
            then(dve.tensor_tensor(top1[:], top1[:], total[:], ALU.mult))
            then(dve.tensor_tensor(top2[:], top2[:], total[:], ALU.mult))
            then(dve.tensor_tensor(hot1[:], hot1[:], wide(top1), ALU.mult))
            then(dve.tensor_tensor(hot2[:], hot2[:], wide(top2), ALU.mult))
            then(dve.tensor_tensor(wts[:, :, 1:NE], hot1[:], hot2[:], ALU.add))

        @block.tensor
        def _(pe):
            pe.wait_ge(const_ready, 6 + ER)

            def turn(dst, src):
                for c in range(DC):
                    for a in range(2):
                        at = c * 256 + a * P
                        last = pe.transpose(dst[:, at:at + P], src[:, a, c * P:(c + 1) * P], ident[:])
                last.then_inc(t_ready, 1)

            with pe.Fori(0, NBLK) as t:
                pe.wait_ge(y_in, t * DMA + DMA)
                for s in range(TT):
                    if s >= 2:
                        pe.wait_ge(y_used, t * TT + (s - 1))
                    for g in range(NG):
                        last = pe.transpose(psY[s % 2][:, g * P:(g + 1) * P], yT[:, g, s * P:(s + 1) * P], ident[:])
                    last.then_inc(y_ready, 1)
                for i in range(2):
                    pe.wait_ge(y_used, t * TT + 2 * (i + 1))
                    turn(psT[i], yn[:, 2 * i:2 * i + 2, :])
                pe.wait_ge(w_ready, 2)
                for i in range(2):
                    pe.wait_ge(t_used, t * 4 + (i + 1))
                    for a in range(2):
                        s = 2 * i + a
                        for c in range(DC):
                            last = pe.matmul(psW[i][:, a * D:(a + 1) * D], ynT[:, c, s * P:(s + 1) * P], wo[:, c, :],
                                             start=c == 0, stop=c == DC - 1)
                    last.then_inc(o_ready, 1)
                for i in range(2):
                    pe.wait_ge(xn_ready, t * TT + 2 * (i + 1))
                    turn(psT[i], xn[:, 2 * i:2 * i + 2, :])
                pe.wait_ge(t_used, t * 4 + 4)
                for s in range(TT):
                    for c in range(DC):
                        last = pe.matmul(psL[:, 8 * s:8 * s + ER], xnT[:, c, s * P:(s + 1) * P], wr[:, c, :],
                                         start=c == 0, stop=c == DC - 1)
                last.then_inc(l_ready, 1)


def experts(nc, x12, xT2, wts, w_ln2, Wg_s, Wu_s, Wd_s, Wg_r, Wu_r, Wd_r, out):
    GU = 2 * NE
    with ExitStack() as ctx:
        def sb(name, shape, dt=F32):
            return ctx.enter_context(nc.sbuf_tensor("ex_" + name, shape, dt))

        def ps(name):
            return ctx.enter_context(nc.psum_tensor("ex_" + name, [P, HALF], F32))

        def sem(name):
            return ctx.enter_context(nc.semaphore("ex_" + name))

        wg, wu, wd = (sb(n, [P, NE, DC, D]) for n in ("wg", "wu", "wd"))
        ln2 = sb("ln2e", [P, DC])
        eps, mhalf = sb("eps5", [P, TT]), sb("mhalf5", [P, TT])
        xT = [sb(f"xTe{i}", [P, DC, HALF]) for i in range(2)]
        acc = [sb(f"acc{i}", [P, TT, D]) for i in range(2)]
        sg = sb("sg", [P, 4, HALF])
        h = [sb(f"he{i}", [P, DC, HALF]) for i in range(2)]
        bst, mv = sb("bst5", [P, TT, 6]), sb("mv5", [P, TT, 2])
        ve, rstd = sb("ve5", [P, TT]), sb("rstd5", [P, TT])
        psG, psU = ([ps(f"{n}{i}") for i in range(2)] for n in ("psG", "psU"))
        psD = [ps(f"psD{i}") for i in range(4)]

        w_in, turn = sem("w5_in"), sem("turn5")
        x_in, a_in = [sem(f"xTe_in{i}") for i in range(2)], [sem(f"acc_in{i}") for i in range(2)]
        out_done = [sem(f"out_done{i}") for i in range(2)]
        const_ready, w_ready = sem("const5_ready"), sem("w5_ready")
        gu_ready, sg_ready, h_ready = sem("gu_ready"), sem("sg_ready"), sem("h5_ready")
        d_ready, acc_step = sem("down_ready"), sem("acc_step")
        st_step, mv_ready, rs_step, rs_ready, o_ready = (sem(n) for n in (
            "st5_step", "mv5_ready", "rs5_step", "rs5_ready", "ln5_ready"))

        block = ctx.enter_context(nc.Block())

        def rows(t_dram, b, q):
            return t_dram[b].rearrange("(h s p) d -> h p s d", h=NH, p=P)[q]

        @block.sync
        def _(sp):
            for q in range(NH):
                sp.dma_start(xT[q][:], xT2[q]).then_inc(x_in[q], DMA)
            for w, shared, routed in ((wg, Wg_s, Wg_r), (wu, Wu_s, Wu_r), (wd, Wd_s, Wd_r)):
                sp.dma_start(w[:, 0], shared.rearrange("(c p) n -> p c n", p=P)).then_inc(w_in, DMA)
                for e in range(ER):
                    sp.dma_start(w[:, e + 1], routed[e].rearrange("(c p) n -> p c n", p=P)).then_inc(w_in, DMA)
            sp.dma_start(ln2[:], w_ln2.rearrange("(c p) -> p c", p=P), allow_slow_non_contiguous=True).then_inc(w_in, DMA)
            for q in range(NH):
                sp.dma_start(acc[q][:], rows(x12, 0, q)).then_inc(a_in[q], DMA)

            def body(b, last):
                for q in range(NH):
                    if q == 0:
                        if not (isinstance(b, int) and b == 0):
                            store(b - 1, 1)
                            sp.wait_ge(out_done[1], b * DMA)
                            sp.sem_inc(turn, 1)
                            sp.dma_start(acc[1][:], rows(x12, b, 1)).then_inc(a_in[1], DMA)
                    else:
                        store(b, 0)
                        if not last:
                            sp.wait_ge(out_done[0], b * DMA + DMA)
                            sp.sem_inc(turn, 1)
                            sp.dma_start(acc[0][:], rows(x12, b + 1, 0)).then_inc(a_in[0], DMA)
                    if not last:
                        sp.wait_ge(gu_ready, b * (2 * GU) + (q + 1) * GU)
                        sp.sem_inc(turn, 1)
                        sp.dma_start(xT[q][:], xT2[b * NH + (q + NH)]).then_inc(x_in[q], DMA)

            def store(b, q):
                sp.wait_ge(o_ready, b * NH + (q + 1))
                sp.sem_inc(turn, 1)
                sp.dma_start(rows(out, b, q), acc[q][:]).then_inc(out_done[q], DMA)

            body(0, False)
            with sp.Fori(1, B - 1) as b:
                body(b, False)
            body(B - 1, True)
            store(B - 1, 1)
            for q in range(NH):
                sp.wait_ge(out_done[q], B * DMA)

        @block.gpsimd
        def _(pool):
            pool.memset(eps[:], LN_EPS).then_inc(const_ready, 1)
            pool.memset(mhalf[:], -0.5).then_inc(const_ready, 1)
            pool.wait_ge(const_ready, 2)
            with pool.Fori(0, NBLK) as t:
                pool.wait_ge(mv_ready, t * TT + TT)
                pool.tensor_tensor(ve[:], mv[:, :, 1], eps[:], ALU.add).then_inc(rs_step, 1)
                pool.wait_ge(rs_step, t + 1)
                pool.tensor_tensor(rstd[:], ve[:], mhalf[:], ALU.pow).then_inc(rs_ready, 1)

        @block.scalar
        def _(act):
            def body(b, first):
                for n in range(2 * GU):
                    act.wait_ge(gu_ready, b * (2 * GU) + (n + 1))
                    if not (first and n < 4):
                        act.wait_ge(h_ready, b * (2 * GU) + (n - 3))
                    nc.scalar.activation(sg[:, n % 4, :], psG[n % 2][:], ACT.Silu).then_inc(sg_ready, 1)

            body(0, True)
            with act.Fori(1, B) as b:
                body(b, False)

        @block.vector
        def _(dve):
            dve.wait_ge(w_in, (3 * NE + 1) * DMA)
            for e in range(NE):
                for w in (wg, wu):
                    for c in range(DC):
                        dve.tensor_scalar(w[:, e, c, :], w[:, e, c, :], ln2[:, c:c + 1], None, ALU.mult).then_inc(w_ready, 1)

            def hidden(b, q, e, first):
                for ic in range(DC):
                    n = (q * NE + e) * 2 + ic
                    dve.wait_ge(sg_ready, b * (2 * GU) + (n + 1))
                    if not (first and n < 4):
                        dve.wait_ge(d_ready, b * (2 * GU) + (2 * (n // 2) - 2))
                    dve.tensor_tensor(h[e % 2][:, ic, :], sg[:, n % 4, :], psU[ic][:], ALU.mult).then_inc(h_ready, 1)

            def gather(b, q, e):
                for i in range(2):
                    n = (q * NE + e) * 2 + i
                    dve.wait_ge(d_ready, b * (2 * GU) + (n + 1))
                    if e == 0:
                        dve.wait_ge(a_in[q], b * DMA + DMA)
                    else:
                        dve.wait_ge(acc_step, b * (4 * GU) + 2 * (n - 2) + 2)
                    for a in range(2):
                        s = 2 * i + a
                        dve.scalar_tensor_tensor(acc[q][:, s, :], psD[n % 4][:, a * D:(a + 1) * D],
                                                 wts[:, b * (NH * TT) + (q * TT + s), e:e + 1], acc[q][:, s, :],
                                                 ALU.mult, ALU.add).then_inc(acc_step, 1)

            def statistics(b, q):
                dve.wait_ge(acc_step, b * (4 * GU) + (q + 1) * 2 * GU)
                for s in range(TT):
                    dve.bn_stats(bst[:, s, :], acc[q][:, s, :]).then_inc(st_step, 1)

            def aggregate(b, q):
                for s in range(TT):
                    dve.bn_aggr(mv[:, s, :], bst[:, s, :]).then_inc(mv_ready, 1)

            def normalise(b, q):
                dve.wait_ge(rs_ready, b * NH + (q + 1))
                for s in range(TT):
                    last = dve.tensor_scalar(acc[q][:, s, :], acc[q][:, s, :], mv[:, s, 0:1], rstd[:, s:s + 1],
                                             ALU.subtract, ALU.mult)
                last.then_inc(o_ready, 1)

            def step(b, q, e, first, last):
                bn, qn, en = (b, q, e + 1) if e + 1 < NE else (b, q + 1, 0)
                if qn == NH:
                    bn, qn = b + 1, 0
                if not (last and qn == 0 and q == 1):
                    hidden(bn, qn, en, first and q == 0 and qn == 0)
                before = (b, 0) if q else (b - 1, 1)
                if not (first and q == 0):
                    if e == 1:
                        statistics(*before)
                        dve.wait_ge(st_step, before[0] * (NH * TT) + (before[1] + 1) * TT)
                gather(b, q, e)
                if not (first and q == 0):
                    if e == 1:
                        aggregate(*before)
                    if e == 3:
                        normalise(*before)

            def body(b, first, last):
                for q in range(NH):
                    for e in range(NE):
                        step(b, q, e, first, last)

            hidden(0, 0, 0, True)
            body(0, True, False)
            with dve.Fori(1, B - 1) as b:
                body(b, False, False)
            body(B - 1, False, True)
            statistics(B - 1, 1)
            dve.wait_ge(st_step, B * NH * TT)
            aggregate(B - 1, 1)
            normalise(B - 1, 1)

        @block.tensor
        def _(pe):
            def gate_up(b, q, e, first):
                pe.wait_ge(x_in[q], b * DMA + DMA)
                for ic in range(DC):
                    n = (q * NE + e) * 2 + ic
                    if not (first and n < 2):
                        pe.wait_ge(h_ready, b * (2 * GU) + (n - 1))
                    for ps_, w in ((psG, wg), (psU, wu)):
                        for c in range(DC):
                            last = pe.matmul(ps_[ic][:], w[:, e, c, ic * P:(ic + 1) * P], xT[q][:, c, :],
                                             start=c == 0, stop=c == DC - 1)
                    last.then_inc(gu_ready, 1)

            def down(b, q, e, first):
                pe.wait_ge(h_ready, b * (2 * GU) + ((q * NE + e) * 2 + 2))
                for i in range(2):
                    n = (q * NE + e) * 2 + i
                    if not (first and n < 4):
                        pe.wait_ge(acc_step, b * (4 * GU) + 2 * (n - 4) + 2)
                    for a in range(2):
                        s = 2 * i + a
                        for ic in range(DC):
                            last = pe.matmul(psD[n % 4][:, a * D:(a + 1) * D], h[e % 2][:, ic, s * P:(s + 1) * P],
                                             wd[:, e, ic, :], start=ic == 0, stop=ic == DC - 1)
                    last.then_inc(d_ready, 1)

            def body(b, first, last):
                for q in range(NH):
                    for e in range(NE):
                        bn, qn, en = (b, q, e + 1) if e + 1 < NE else (b, q + 1, 0)
                        if qn == NH:
                            bn, qn = b + 1, 0
                        if not (last and qn == 0 and q == 1):
                            gate_up(bn, qn, en, first and q == 0 and qn == 0)
                        down(b, q, e, first and q == 0)

            pe.wait_ge(w_ready, 4 * NE)
            gate_up(0, 0, 0, True)
            body(0, True, False)
            with pe.Fori(1, B - 1) as b:
                body(b, False, False)
            body(B - 1, False, True)


def layer(nc, out, rope, x, Wq, bq, Wk, bk, Wv, bv, Wo, bo, w_ln1, w_ln2, W_kvd, W_qd, W_ku, W_qu, W_vu,
          W_ropeq, W_ropek, W_o, Wg_s, Wu_s, Wd_s, Wg_r, Wu_r, Wd_r, W_router, routing_bias):
    def scratch(name, shape, dt=F32):
        return nc.dram_tensor(name, shape, dt, kind="Internal").ap()

    x1, x12 = scratch("x1_rows", [B, S, D]), scratch("x1_x2_rows", [B, S, D])
    zd = scratch("z_rows", [HEADS, S])
    qp, kp = scratch("q_parts", [B, 3, D, S], BF16), scratch("k_parts", [B, 3, D, S], BF16)
    v_rows = scratch("v_rows", [B, S, MH * VW])
    y_cols = scratch("y_cols", [B, NH, NG, P, HALF])
    xT2 = scratch("x2_norm_cols", [NBLK, P, DC, HALF])

    linear_attention(nc, x, Wq, bq, Wk, bk, Wv, bv, Wo, bo, x1, zd)
    latent_projections(nc, x1, w_ln1, W_kvd, W_qd, W_ku, W_qu, W_vu, W_ropeq, W_ropek, rope, qp, kp, v_rows)
    softmax_attention(nc, qp, kp, v_rows, y_cols)
    with nc.sbuf_tensor("wts", [P, NBLK * TT, NE], F32) as wts:
        output_and_router(nc, y_cols, x1, W_o, w_ln2, W_router, routing_bias, x12, xT2, wts)
        experts(nc, x12, xT2, wts, w_ln2, Wg_s, Wu_s, Wd_s, Wg_r, Wu_r, Wd_r, out)


_ATTN = ["x", "Wq", "bq", "Wk", "bk", "Wv", "bv", "Wo", "bo"]
_FFN = ["w_ln1", "w_ln2", "W_kvd", "W_qd", "W_ku", "W_qu", "W_vu", "W_ropeq", "W_ropek", "W_o",
        "Wg_s", "Wu_s", "Wd_s", "Wg_r", "Wu_r", "Wd_r", "W_router", "routing_bias"]


def kernel(**inputs):
    import concourse.bacc as _bacc
    from concourse.bass_utils import run_bass_kernel_spmd as _run

    nc = _bacc.Bacc("TRN2", target_bir_lowering=False, num_devices=1)
    arrays = {"in_rope_dram": rope_table()}
    names = ["in_rope_dram"]
    for prefix, group in (("L0_attn_", _ATTN), ("L0_ffn_", _FFN)):
        for name in group:
            arrays[f"in_{prefix}{name}_dram"] = np.ascontiguousarray(inputs[prefix + name])
            names.append(f"in_{prefix}{name}_dram")
    args = [nc.dram_tensor("out_dram", (B, S, D), F32, kind="ExternalOutput").ap()]
    for name in names:
        a = arrays[name]
        args.append(nc.dram_tensor(name, a.shape, mybir.dt.from_np(a.dtype), kind="ExternalInput").ap())
    layer(nc, *args)
    r = _run(nc, [arrays], core_ids=[0])
    return r.results[0]["out_dram"]
```

```python
from contextlib import ExitStack

import concourse.bass as bass
import concourse.mybir as mybir
import numpy as np

ALU = mybir.AluOpType
ACT = mybir.ActivationFunctionType
AX = mybir.AxisListType
F32 = mybir.dt.float32
BF16 = mybir.dt.bfloat16
F32R = mybir.dt.float32r

P = 128
B, S, D = 4, 1024, 256
DC = D // P
ST = S // P
HALF = 512
NH = S // HALF
HEADS, HD = 16, 64
PAIRS = HEADS * HD // P
LN_EPS = 1e-5
Z_EPS = 1e-6
DMA = 16


def linear_attention(nc, x, Wq, bq, Wk, bk, Wv, bv, Wo, bo, x1, zd):
    XW = D + 1
    STEPS = PAIRS + 3
    ring_x = []
    for s in range(STEPS):
        if s < PAIRS:
            ring_x.append(("kx", s))
        if s >= 3:
            ring_x.append(("m", s - 3))
    ring_x += [("out", t) for t in range(ST)]
    X_OF = {use: i for i, use in enumerate(ring_x)}
    XN = len(ring_x)
    XP = PAIRS
    TK = ST // 2
    KN = ST * NH
    AN = TK + KN
    assert XN % 2 == 0 and AN % 2 == 0 and XP % 2 == 0

    with ExitStack() as ctx:
        def sb(name, shape, dt=F32):
            return ctx.enter_context(nc.sbuf_tensor(name, shape, dt))

        def ps(name):
            return ctx.enter_context(nc.psum_tensor(name, [P, HALF], F32))

        def sem(name):
            return ctx.enter_context(nc.semaphore(name))

        wq_hi, wq_lo, wk_hi, wk_lo = (sb(n, [P, DC, HEADS * HD], F32R) for n in ("wq_hi", "wq_lo", "wk_hi", "wk_lo"))
        wv = sb("wv", [P, DC, HEADS * HD])
        wo = sb("wo", [P, PAIRS, D])
        ident = sb("ident1", [P, P])
        bq_c = sb("bq_c", [P, PAIRS])
        bq1_c = sb("bq1_c", [P, PAIRS])
        bv_c = sb("bv_c", [P, PAIRS])
        bk1 = sb("bk1", [P, HEADS * HD])
        bo_b = sb("bo_b", [P, D])
        neg1 = sb("neg1", [P, 1])
        bvwo = sb("bvwo", [P, PAIRS, D])
        xs = sb("xs", [P, ST, XW])
        xT_hi, xT_lo = sb("xT_hi", [P, DC, S], F32R), sb("xT_lo", [P, DC, S], F32R)
        qf = sb("qf", [P, PAIRS, S])
        kf = sb("kf", [P, ST, HEADS * HD])
        wq, wk = qf[:, 0:DC, :], kf[:, 0:DC, :]
        ke, ku = sb("ke", [P, 4, HALF]), sb("ku", [P, 4, HALF])
        qe, qu = ke, ku
        kx = sb("kx", [P, PAIRS, XW])
        kxT = sb("kxT", [P, 2, DC, P])
        kvT = sb("kvT", [P, 2, P])
        mm = kx[:, :, 0:D]
        ksb = sb("ksb", [P, PAIRS, 32])
        den = sb("den", [P, HALF // 2])
        z = sb("z", [P, HALF // 2])
        zb = sb("zb", [P, 4, S])
        bvr = zb[:, 0, :].rearrange("p (a d) -> p a d", a=PAIRS)
        res = sb("res", [P, ST, D])
        h = res
        bst = sb("bst", [P, ST, 6])
        mv = sb("mv", [P, ST, 2])
        ve, rstd, mhalf = sb("ve", [P, ST]), sb("rstd", [P, ST]), sb("mhalf", [P, ST])

        eps = sb("eps", [P, ST])

        psA = [ps(f"psA{i}") for i in range(2)]
        psQ = [ps(f"psQ{i}") for i in range(2)]
        psX = [ps(f"psX{i}") for i in range(2)]
        psT, psV = ps("psT"), ps("psV")

        k_in, q_in, o_in = sem("k_in"), sem("q_in"), sem("o_in")
        x_in = sem("x_in")
        r_in = sem("r_in")
        z_out, z_back = sem("z_out"), [sem(f"z_back{i}") for i in range(4)]
        st_done = sem("st_done")
        const_ready = sem("const_ready")
        bias_ready = sem("bias_ready")
        w_hi_ready, w_lo_ready, xh_ready = sem("w_hi_ready"), sem("w_lo_ready"), sem("xT_hi_ready")
        a_ready, a_used = sem("a_ready"), sem("a_used")
        q_ready, q_free = sem("q_ready"), sem("q_free")
        qe_free = sem("qe_free")
        x_ready, x_used = sem("x_ready"), sem("x_used")
        t_ready, kxt_ready = sem("t_ready"), sem("kxt_ready")
        v_ready, kvt_ready = sem("v_ready"), sem("kvt_ready")
        d_ready, ksb_ready = sem("d_ready"), sem("ksb_ready")
        e_ready, kf_ready = sem("e_ready"), sem("kf_ready")
        z_step, z_ready = sem("z_step"), sem("z_ready")
        zb_free = [sem(f"zb_free{i}") for i in range(4)]
        h_free, h_step, mv_ready = sem("h_free"), sem("h_step"), sem("mv_ready")
        stats_seen = sem("stats_seen")
        rs_step, rs_ready, h_ready = sem("rs_step"), sem("rs_ready"), sem("h_ready")
        r_ready = sem("r_ready")

        block = ctx.enter_context(nc.Block())

        def scale_q(engine, b, p):
            engine.wait_ge(z_back[p % 4], b * (2 * DMA) + (p // 4 + 1) * DMA)
            engine.tensor_tensor(qf[:, p, :], qf[:, p, :], zb[:, p % 4, :], ALU.mult).then_inc(zb_free[p % 4], 1)

        @block.sync
        def _(sp):
            sp.dma_start(xs[:, :, 0:D], x[0].rearrange("(s t) d -> t s d", t=P)).then_inc(x_in, DMA)
            sp.dma_start(wk, Wk.rearrange("(c p) h d -> p c (h d)", p=P)).then_inc(k_in, DMA)
            sp.dma_start(bk1[:], bk.rearrange("h d -> (h d)").partition_broadcast(P)).then_inc(k_in, DMA)
            sp.dma_start(wq, Wq.rearrange("(c p) h d -> p c (h d)", p=P)).then_inc(q_in, DMA)
            sp.dma_start(wv[:], Wv.rearrange("(c p) h d -> p c (h d)", p=P)).then_inc(o_in, DMA)
            sp.dma_start(wo[:], Wo.rearrange("(a b) m d -> (b m) a d", b=2)).then_inc(o_in, DMA)
            for dst, v, landed in ((bq_c, bq, q_in), (bv_c, bv, o_in)):
                sp.dma_start(dst[:], v.rearrange("(a b) m -> (b m) a", b=2),
                             allow_slow_non_contiguous=True).then_inc(landed, DMA)
            sp.dma_start(bo_b[:], bo.partition_broadcast(P)).then_inc(o_in, DMA)
            sp.sem_inc(h_free, 1)

            def batch(b, last):
                sp.wait_ge(x_used, b * XN + XP)
                sp.dma_start(res[:], x[b].rearrange("(s t) d -> t s d", t=P)).then_inc(r_in, DMA)
                if not last:
                    sp.wait_ge(x_ready, b * XN + (XP + X_OF[("kx", PAIRS - 1)] + 1))
                    sp.dma_start(xs[:, :, 0:D], x[b + 1].rearrange("(s t) d -> t s d", t=P)).then_inc(x_in, DMA)
                sp.wait_ge(z_ready, b + 1)
                for j in range(4):
                    sp.dma_start(zd[:, j * 256:(j + 1) * 256], z[32 * j:32 * j + HEADS, :]).then_inc(z_out, DMA)
                sp.wait_ge(z_out, b * (4 * DMA) + 4 * DMA)
                for p in range(PAIRS):
                    sp.wait_ge(zb_free[p % 4], b * 2 + (p // 4 + 1))
                    src = zd[2 * p:2 * p + 2, :].unsqueeze(1).broadcast_to([2, HD, S])
                    sp.dma_start(zb[:, p % 4, :], src).then_inc(z_back[p % 4], DMA)
                sp.wait_ge(h_ready, b + 1)
                sp.dma_start(x1[b].rearrange("(s t) d -> t s d", t=P), h[:]).then_inc(st_done, DMA)
                sp.wait_ge(st_done, b * DMA + DMA)
                sp.sem_inc(h_free, 1)

            with sp.Fori(0, B - 1) as b:
                batch(b, False)
            batch(B - 1, True)

        @block.gpsimd
        def _(pool):
            pool.memset(ident[:], 0.0).then_inc(const_ready, 1)
            pool.memset(xs[:, :, D:XW], 1.0).then_inc(const_ready, 1)
            pool.memset(ksb[:], 0.0).then_inc(const_ready, 1)
            pool.memset(kvT[:], 0.0).then_inc(const_ready, 1)
            pool.memset(bvr, 0.0).then_inc(const_ready, 1)
            pool.memset(mhalf[:], -0.5).then_inc(const_ready, 1)
            pool.memset(eps[:], LN_EPS).then_inc(const_ready, 1)
            pool.memset(neg1[:], -1.0).then_inc(const_ready, 1)
            pool.wait_ge(const_ready, 8)
            pool.affine_select(out=ident[:], in_=ident[:], compare_op=ALU.not_equal, fill=1.0, base=0,
                               pattern=[[-1, P]], channel_multiplier=1).then_inc(const_ready, 1)
            pool.wait_ge(o_in, 4 * DMA)

            def batch(b, last):
                pool.wait_ge(r_in, b * DMA + DMA)
                pool.tensor_tensor(res[:], res[:], bo_b[:].unsqueeze(1).broadcast_to([P, ST, D]),
                                   ALU.add).then_inc(r_ready, 1)
                for p in range(PAIRS):
                    if (p % 4 >= 2 if last else p % 4 < 3):
                        scale_q(pool, b, p)
                pool.wait_ge(mv_ready, b * ST + ST)
                pool.tensor_tensor(ve[:], mv[:, :, 1], eps[:], ALU.add).then_inc(rs_step, 1)
                pool.wait_ge(rs_step, b + 1)
                pool.tensor_tensor(rstd[:], ve[:], mhalf[:], ALU.pow).then_inc(rs_ready, 1)

            with pool.Fori(0, B - 1) as b:
                batch(b, False)
            batch(B - 1, True)

        @block.scalar
        def _(act):
            act.sem_inc(q_free, 2)

            def k_exp(b):
                for n in range(KN):
                    act.wait_ge(a_used, b * AN + (TK + n + 1))
                    nc.scalar.activation(ke[:, n % 4, :], ku[:, n % 4, :], ACT.Exp, bias=neg1[:]).then_inc(e_ready, 1)
                    if isinstance(b, int) and b == 0 and n == KN // 2:
                        act.wait_ge(q_in, 2 * DMA)
                        nc.scalar.copy(wq_hi[:], wq).then_inc(w_hi_ready, 1)

            act.wait_ge(k_in, 2 * DMA)
            nc.scalar.copy(wk_hi[:], wk).then_inc(w_hi_ready, 1)
            act.wait_ge(const_ready, 9)
            k_exp(0)
            act.wait_ge(bias_ready, 4)
            act.wait_ge(kf_ready, KN)

            def batch(b, last):
                for n in range(KN):
                    p = n // NH
                    act.wait_ge(q_ready, b * KN + (n + 1))
                    act.wait_ge(qe_free, b * KN + (n + 1))
                    nc.scalar.activation(qe[:, n % 4, :], psQ[n % 2][:], ACT.Exp, bias=bq_c[:, p:p + 1])
                    nc.scalar.activation(qu[:, n % 4, :], psQ[n % 2][:], ACT.Identity,
                                         bias=bq1_c[:, p:p + 1]).then_inc(q_free, 1)
                for s in range(STEPS):
                    if 0 <= s - 1 < PAIRS:
                        p = s - 1
                        act.wait_ge(t_ready, b * PAIRS + (p + 1))
                        nc.scalar.copy(kxT[:, p % 2, :, :].rearrange("p c d -> p (c d)"),
                                       psT[:, 0:DC * P]).then_inc(kxt_ready, 1)
                    if 0 <= s - 2 < PAIRS:
                        p = s - 2
                        act.wait_ge(v_ready, b * PAIRS + (p + 1))
                        nc.scalar.copy(kvT[0:HD, p % 2, 0:HD], psV[0:HD, 0:HD])
                        nc.scalar.copy(kvT[HD:P, p % 2, HD:P], psV[HD:P, HD:P]).then_inc(kvt_ready, 1)
                act.wait_ge(x_used, b * XN + (XP + X_OF[("kx", PAIRS - 1)] + 1))
                flat = ksb[:].rearrange("p a h -> p (a h)")
                for i in range(2):
                    rows = slice(HD * i, HD * i + HD)
                    nc.scalar.copy(flat[rows, i:i + 34 * (PAIRS - 1) + 1:34], kx[rows, :, D]).then_inc(ksb_ready, 1)
                if not last:
                    k_exp(b + 1)

            with act.Fori(0, B - 1) as b:
                batch(b, False)
            batch(B - 1, True)

        @block.vector
        def _(dve):
            dve.sem_inc(qe_free, 4)
            for i in range(4):
                dve.sem_inc(zb_free[i], 1)
            def turned_x(b):
                for n in range(TK):
                    dve.wait_ge(a_ready, b * AN + (n + 1))
                    cols, src = slice(n * 256, (n + 1) * 256), psA[n % 2][:].rearrange("p (c t) -> p c t", c=DC)
                    dve.tensor_copy(xT_hi[:, :, cols], src).then_inc(xh_ready, 1)
                    dve.wait_ge(xh_ready, b * TK + (n + 1))
                    dve.tensor_tensor(xT_lo[:, :, cols], src, xT_hi[:, :, cols], ALU.subtract).then_inc(a_used, 1)

            turned_x(0)
            dve.wait_ge(k_in, 2 * DMA)
            dve.tensor_scalar(bk1[:], bk1[:], 1.0, None, ALU.add).then_inc(bias_ready, 1)
            dve.wait_ge(w_hi_ready, 1)
            dve.tensor_tensor(wk_lo[:], wk, wk_hi[:], ALU.subtract).then_inc(w_lo_ready, 1)
            dve.wait_ge(bias_ready, 1)

            def other_weights():
                dve.wait_ge(w_hi_ready, 2)
                dve.tensor_tensor(wq_lo[:], wq, wq_hi[:], ALU.subtract).then_inc(w_lo_ready, 1)
                dve.tensor_scalar(bq1_c[:], bq_c[:], 1.0, None, ALU.add).then_inc(bias_ready, 1)
                dve.wait_ge(o_in, 4 * DMA)
                dve.wait_ge(const_ready, 9)
                for i in range(2):
                    rows = slice(HD * i, HD * i + HD)
                    dve.tensor_copy(bvr[rows, :, HD * i:HD * i + HD],
                                    bv_c[rows, :].unsqueeze(2).broadcast_to([HD, PAIRS, HD])).then_inc(bias_ready, 1)

            def k_features(b, z_of=None):
                if z_of is not None:
                    dve.wait_ge(qe_free, z_of * KN + (KN + 4))

                def finish(n):
                    dve.wait_ge(e_ready, b * KN + (n + 1))
                    out = kf[:, n // NH, (n % NH) * HALF:(n % NH + 1) * HALF]
                    dve.scalar_tensor_tensor(out, ke[:, n % 4, :], 1.0, ku[:, n % 4, :],
                                             ALU.min, ALU.max).then_inc(kf_ready, 1)

                for n in range(KN):
                    dve.wait_ge(a_ready, b * AN + (TK + n + 1))
                    if n >= 4 or z_of is not None:
                        dve.wait_ge(kf_ready, b * KN + (n - 3))
                    cols = slice((n % NH) * HALF, (n % NH + 1) * HALF)
                    dve.tensor_tensor(ku[:, n % 4, :], psA[(TK + n) % 2][:], bk1[:, cols], ALU.add).then_inc(a_used, 1)
                    if n >= 1:
                        finish(n - 1)
                    if z_of is not None and n in (9, 13):
                        scale_q(dve, z_of, n - 6)
                    if z_of is None and n == KN - 3:
                        other_weights()
                finish(KN - 1)

            k_features(0)
            for p in range(PAIRS):
                dve.wait_ge(x_ready, p + 1)
                dve.tensor_copy(bvwo[:, p, :], psX[p % 2][:, 0:D]).then_inc(x_used, 1)

            def batch(b, last):
                for n in range(KN):
                    p, half = n // NH, n % NH
                    dve.wait_ge(q_free, b * KN + (n + 3))
                    dve.scalar_tensor_tensor(qf[:, p, half * HALF:(half + 1) * HALF], qe[:, n % 4, :], 1.0,
                                             qu[:, n % 4, :], ALU.min, ALU.max).then_inc(qe_free, 1)
                for i, (what, p) in enumerate(ring_x[:2 * PAIRS]):
                    dve.wait_ge(x_ready, b * XN + (XP + i + 1))
                    if what == "kx":
                        dve.tensor_copy(kx[:, p, :], psX[i % 2][:, 0:XW]).then_inc(x_used, 1)
                    else:
                        dve.scalar_tensor_tensor(mm[:, p, :], bvwo[:, p, :], kx[:, p, D:XW], psX[i % 2][:, 0:D],
                                                 ALU.mult, ALU.add).then_inc(x_used, 1)
                if not last:
                    turned_x(b + 1)
                dve.wait_ge(d_ready, b + 1)
                dve.tensor_scalar(den[:], psV[:, 0:HALF // 2], Z_EPS, None, ALU.add).then_inc(z_step, 1)
                dve.wait_ge(z_step, b + 1)
                dve.reciprocal(z[:], den[:]).then_inc(z_ready, 1)
                if not last:
                    k_features(b + 1, z_of=b)
                else:
                    for p in range(PAIRS):
                        if p % 4 < 2:
                            scale_q(dve, b, p)
                dve.wait_ge(r_ready, b + 1)
                dve.wait_ge(h_free, b + 1)
                for t in range(ST + 2):
                    if t < ST:
                        i = X_OF[("out", t)]
                        dve.wait_ge(x_ready, b * XN + (XP + i + 1))
                        dve.tensor_tensor(h[:, t, :], psX[i % 2][:, 0:D], res[:, t, :], ALU.add).then_inc(x_used, 1)
                    if 1 <= t <= ST:
                        dve.wait_ge(x_used, b * XN + (XP + X_OF[("out", t - 1)] + 1))
                        if t >= 2:
                            dve.wait_ge(h_step, b * ST + (t - 1))
                        dve.bn_stats(bst[:, t - 1, :], h[:, t - 1, :]).then_inc(h_step, 1)
                    if t >= 2:
                        if t == ST + 1:
                            dve.wait_ge(h_step, b * ST + ST)
                            dve.sem_inc(stats_seen, 1)
                        dve.bn_aggr(mv[:, t - 2, :], bst[:, t - 2, :]).then_inc(mv_ready, 1)
                dve.wait_ge(rs_ready, b + 1)
                for t in range(ST):
                    last_op = dve.tensor_scalar(h[:, t, :], h[:, t, :], mv[:, t, 0:1], rstd[:, t:t + 1],
                                                ALU.subtract, ALU.mult)
                last_op.then_inc(h_ready, 1)

            with dve.Fori(0, B - 1) as b:
                batch(b, False)
            batch(B - 1, True)

        @block.tensor
        def _(pe):
            pe.wait_ge(const_ready, 9)

            def product(dst, hi, lo, m_hi, m_lo):
                for c in range(DC):
                    pe.matmul(dst, hi(c), m_hi(c), start=c == 0, stop=False)
                    pe.matmul(dst, hi(c), m_lo(c), start=False, stop=False)
                    last = pe.matmul(dst, lo(c), m_hi(c), start=False, stop=c == DC - 1)
                return last

            def turn_x(b, first, pairs=range(TK)):
                pe.wait_ge(x_in, b * DMA + DMA)
                for n in pairs:
                    if not (first and n < 2):
                        pe.wait_ge(a_used, b * AN + (n - 1))
                    for c in range(DC):
                        for j in range(2):
                            at = (c * 2 + j) * P
                            last = pe.transpose(psA[n % 2][:, at:at + P], xs[:, 2 * n + j, c * P:(c + 1) * P], ident[:])
                    last.then_inc(a_ready, 1)

            def k_product(b):
                for n in range(KN):
                    s, half = n // NH, n % NH
                    pe.wait_ge(a_used, b * AN + max(TK + n - 1, TK if n == 0 else 0))
                    tok, cols = slice(s * P, (s + 1) * P), slice(half * HALF, (half + 1) * HALF)
                    product(psA[(TK + n) % 2][:], lambda c: xT_hi[:, c, tok], lambda c: xT_lo[:, c, tok],
                            lambda c: wk_hi[:, c, cols], lambda c: wk_lo[:, c, cols]).then_inc(a_ready, 1)

            turn_x(0, True)
            pe.wait_ge(w_lo_ready, 1)
            k_product(0)
            pe.wait_ge(bias_ready, 4)
            for p in range(PAIRS):
                if p >= 2:
                    pe.wait_ge(x_used, p - 1)
                pe.matmul(psX[p % 2][:, 0:D], bvr[:, p, :], wo[:, p, :], start=True, stop=True).then_inc(x_ready, 1)
            pe.wait_ge(w_lo_ready, 2)

            def batch(b, last_batch):
                for n in range(KN):
                    p, half = n // NH, n % NH
                    pe.wait_ge(q_free, b * KN + (n + 1))
                    rows, tok = slice(p * P, (p + 1) * P), slice(half * HALF, (half + 1) * HALF)
                    product(psQ[n % 2][:], lambda c: wq_hi[:, c, rows], lambda c: wq_lo[:, c, rows],
                            lambda c: xT_hi[:, c, tok], lambda c: xT_lo[:, c, tok]).then_inc(q_ready, 1)
                pe.wait_ge(kf_ready, b * KN + KN)
                for s in range(STEPS):
                    if s < PAIRS:
                        i = X_OF[("kx", s)]
                        pe.wait_ge(x_used, b * XN + (XP + i - 1))
                        for t in range(ST):
                            last = pe.matmul(psX[i % 2][:, 0:XW], kf[:, t, s * P:(s + 1) * P], xs[:, t, :],
                                             start=t == 0, stop=t == ST - 1)
                        last.then_inc(x_ready, 1)
                    if 0 <= s - 1 < PAIRS:
                        p = s - 1
                        pe.wait_ge(x_used, b * XN + (XP + X_OF[("kx", p)] + 1))
                        if p >= 1:
                            pe.wait_ge(kxt_ready, b * PAIRS + p)
                        for c in range(DC):
                            last = pe.transpose(psT[:, c * P:(c + 1) * P], kx[:, p, c * P:(c + 1) * P], ident[:])
                        last.then_inc(t_ready, 1)
                    if 0 <= s - 2 < PAIRS:
                        p = s - 2
                        pe.wait_ge(kxt_ready, b * PAIRS + (p + 1))
                        if p >= 1:
                            pe.wait_ge(kvt_ready, b * PAIRS + p)
                        for c in range(DC):
                            last = pe.matmul(psV[:, 0:P], wv[:, c, p * P:(p + 1) * P], kxT[:, p % 2, c, :],
                                             start=c == 0, stop=c == DC - 1)
                        last.then_inc(v_ready, 1)
                    if s >= 3:
                        p = s - 3
                        i = X_OF[("m", p)]
                        pe.wait_ge(kvt_ready, b * PAIRS + (p + 1))
                        pe.wait_ge(x_used, b * XN + (XP + i - 1))
                        pe.matmul(psX[i % 2][:, 0:D], kvT[:, p % 2, :], wo[:, p, :],
                                  start=True, stop=True).then_inc(x_ready, 1)
                pe.wait_ge(ksb_ready, b * 2 + 2)
                pe.wait_ge(qe_free, b * KN + (KN + 4))
                for p in range(PAIRS):
                    if p in (0, PAIRS // 2) and not last_batch:
                        turn_x(b + 1, False, range(p // 2, p // 2 + 2))
                    for j in range(4):
                        last = pe.matmul(psV[32 * j:32 * j + 32, 0:256], ksb[:, p, :], qf[:, p, j * 256:(j + 1) * 256],
                                         start=p == 0, stop=p == PAIRS - 1)
                last.then_inc(d_ready, 1)
                if not last_batch:
                    k_product(b + 1)
                pe.wait_ge(x_used, b * XN + (XP + 2 * PAIRS))
                for t in range(ST):
                    i = X_OF[("out", t)]
                    if t >= 1:
                        pe.wait_ge(x_used, b * XN + (XP + i - 1))
                    for p in range(PAIRS):
                        if t == 0:
                            pe.wait_ge(zb_free[p % 4], b * 2 + (p // 4 + 2))
                        last = pe.matmul(psX[i % 2][:, 0:D], qf[:, p, t * P:(t + 1) * P], mm[:, p, :],
                                         start=p == 0, stop=p == PAIRS - 1)
                    last.then_inc(x_ready, 1)

            with pe.Fori(0, B - 1) as b:
                batch(b, False)
            batch(B - 1, True)



MH, MHD, ROPE_W = 16, 16, 8
LAT = 64
QK_ROWS = 96
RMS_EPS = 1e-5
VW = 32


def latent_projections(nc, x1, w_ln1, W_kvd, W_qd, W_ku, W_qu, W_vu, W_ropeq, W_ropek, rope, qp, kp, v_dram):
    K, KR, Q, QR = range(4)
    PE0, PEN = 2, 9
    LATENT, ROPEK, NOPEK, VAL0, VAL1, NOPEQ, ROPEQ, TR0, TR1 = range(9)
    PARTS = 3 * DMA

    with ExitStack() as ctx:
        def sb(name, shape, dt=F32):
            return ctx.enter_context(nc.sbuf_tensor("lp_" + name, shape, dt))

        def sem(name):
            return ctx.enter_context(nc.semaphore("lp_" + name))

        ident = sb("ident2", [P, P])
        stage = sb("stage", [P, 3, P])
        stage_r = sb("stage_r", [P, DC, P])
        w_lat = sb("w_lat", [P, DC, P])
        w_rk = sb("w_rk", [P, DC, P])
        w_up = sb("w_up", [P, 3, P])
        w_v = sb("w_v", [P, D])
        ln1 = sb("ln1", [P, DC])
        cos, sin = sb("cos", [P, S]), sb("sin", [P, S])
        xin, xn = sb("xin", [P, ST, D]), sb("xn", [P, ST, D])
        ssq, rms, rn = sb("ssq", [P, ST]), sb("rms", [P, ST]), sb("rn", [P, ST])
        inv_d, half, eps = sb("inv_d", [P, ST]), sb("half", [P, ST]), sb("eps2", [P, ST])
        xT = sb("xnT", [P, DC, S])
        lat = sb("lat", [P, S])
        rot, t1, t2 = sb("rot", [P, 2, S]), sb("t1", [P, S]), sb("t2", [P, S])
        r1 = sb("r1", [P, 4, S])
        part = sb("part", [P, 4, 3, S], BF16)
        vs = sb("vs", [P, ST, MH, VW])
        ring = [ctx.enter_context(nc.psum_tensor(f"lp_ps{i}", [P, S], F32)) for i in range(4)]

        w_in, x_in = sem("w2_in"), sem("x1_in")
        part_out = [sem(f"part_out{j}") for j in range(4)]
        v_out, turn = sem("v_out"), sem("turn")
        const_ready, w_ready = sem("const2_ready"), sem("w2_ready")
        pe_done, act_rel, dve_rel = sem("pe_done"), sem("act_rel"), sem("dve_rel")
        h_ready, r1_ready, m_ready, l_ready = sem("hi_ready"), sem("r1_ready"), sem("mid_ready"), sem("lo_ready")
        rope_step, rot_ready = sem("rope_step"), sem("rot_ready")
        sq_ready, rms_step, rn_step, xn_ready = sem("sq_ready"), sem("rms_step"), sem("rn_step"), sem("xn_ready")

        block = ctx.enter_context(nc.Block())

        @block.sync
        def _(sp):
            sp.dma_start(xin[:], x1[0].rearrange("(s t) d -> t s d", t=P)).then_inc(x_in, DMA)
            sp.dma_start(ln1[:], w_ln1.rearrange("(c p) -> p c", p=P), allow_slow_non_contiguous=True).then_inc(w_in, DMA)
            sp.dma_start(w_lat[:, :, 0:LAT], W_kvd.rearrange("(c p) l -> p c l", p=P)).then_inc(w_in, DMA)
            sp.dma_start(w_lat[:, :, LAT:P], W_qd.rearrange("(c p) l -> p c l", p=P)).then_inc(w_in, DMA)
            sp.dma_start(stage_r[:], W_ropek.rearrange("(c p) n -> p c n", p=P)).then_inc(w_in, DMA)
            for i, (rows, w) in enumerate(((slice(0, LAT), W_ku), (slice(LAT, P), W_qu), (slice(LAT, P), W_ropeq))):
                sp.dma_start(stage[rows, i, :], w).then_inc(w_in, DMA)
            sp.wait_ge(const_ready, 1)
            sp.dma_start(w_v[0:LAT, :], W_vu).then_inc(w_in, DMA)
            for i, table in enumerate((cos, sin)):
                sp.dma_start(table[:], rope[i].unsqueeze(1).broadcast_to([ROPE_W, MH, S])).then_inc(w_in, DMA)
            for j in range(4):
                sp.sem_inc(part_out[j], 1)
            sp.sem_inc(v_out, 1)

            def load_x(b):
                sp.wait_ge(xn_ready, b * ST)
                sp.sem_inc(turn, 1)
                sp.dma_start(xin[:], x1[b].rearrange("(s t) d -> t s d", t=P)).then_inc(x_in, DMA)

            def batch(b, last):
                def store(j):
                    dst = (kp, kp, qp, qp)[j]
                    rows = slice(P * (j % 2), P * (j % 2) + P)
                    sp.wait_ge(l_ready, b * 4 + (j + 1))
                    for i in range(3):
                        sp.dma_start(dst[b, i, rows, :], part[:, j, i, :]).then_inc(part_out[j], DMA)

                store(K)
                store(KR)
                if not last:
                    load_x(b + 2)
                sp.wait_ge(act_rel, b * 5 + 5)
                sp.dma_start(v_dram[b].rearrange("(s t) d -> t s d", t=P), vs[:].rearrange("p s h m -> p s (h m)")).then_inc(v_out, DMA)
                store(Q)
                store(QR)

            load_x(1)
            with sp.Fori(0, B - 2) as b:
                batch(b, False)
            batch(B - 2, True)
            batch(B - 1, True)
            for j in range(4):
                sp.wait_ge(part_out[j], B * PARTS + 1)
            sp.wait_ge(v_out, B * DMA + 1)

        @block.gpsimd
        def _(pool):
            pool.memset(w_v[:], 0.0).then_inc(const_ready, 1)
            pool.memset(w_up[:], 0.0).then_inc(const_ready, 1)
            pool.memset(ident[:], 0.0).then_inc(const_ready, 1)
            pool.memset(inv_d[:], 1.0 / D).then_inc(const_ready, 1)
            pool.memset(half[:], 0.5).then_inc(const_ready, 1)
            pool.memset(eps[:], RMS_EPS).then_inc(const_ready, 1)
            pool.memset(vs[:], 0.0).then_inc(const_ready, 1)
            pool.wait_ge(const_ready, 7)
            pool.memset(vs[:, :, :, MHD], 1.0).then_inc(const_ready, 1)
            pool.affine_select(out=ident[:], in_=ident[:], compare_op=ALU.not_equal, fill=1.0, base=0,
                               pattern=[[-1, P]], channel_multiplier=1).then_inc(const_ready, 1)

            def norm(b):
                pool.wait_ge(sq_ready, b * ST + ST)
                pool.tensor_tensor(rms[:], ssq[:], inv_d[:], ALU.mult).then_inc(rms_step, 1)
                pool.wait_ge(rms_step, b * 3 + 1)
                pool.tensor_tensor(rms[:], rms[:], half[:], ALU.pow).then_inc(rms_step, 1)
                pool.wait_ge(rms_step, b * 3 + 2)
                pool.tensor_tensor(rms[:], rms[:], eps[:], ALU.add).then_inc(rms_step, 1)

            def batch(b, last):
                for j in range(4):
                    if j == 0 and not last:
                        norm(b + 1)
                    pool.wait_ge(m_ready, b * 4 + (j + 1))
                    pool.tensor_tensor(part[:, j, 2, :], r1[:, j, :], part[:, j, 1, :], ALU.subtract).then_inc(l_ready, 1)

            norm(0)
            with pool.Fori(0, B - 1) as b:
                batch(b, False)
            batch(B - 1, True)

        @block.scalar
        def _(act):
            def squares(b):
                act.wait_ge(x_in, b * DMA + DMA)
                for s in range(ST):
                    nc.scalar.activation(xn[:, s, :], xin[:, s, :], ACT.Square, accum_out=ssq[:, s:s + 1]).then_inc(sq_ready, 1)

            def transposed(b):
                for i in range(2):
                    act.wait_ge(pe_done, b * PEN + (i + 1))
                    nc.scalar.copy(xT[:, :, i * HALF:(i + 1) * HALF],
                                   ring[(TR0 + i) % 3][:].rearrange("p (c t) -> p c t", c=DC)).then_inc(act_rel, 1)

            squares(0)
            transposed(0)
            act.wait_ge(const_ready, 9)

            def high(b, j, src):
                act.wait_ge(part_out[j], b * PARTS + 1)
                nc.scalar.copy(part[:, j, 0, :], src).then_inc(h_ready, 1)

            def batch(b, last):
                act.wait_ge(pe_done, b * PEN + (PE0 + LATENT + 1))
                nc.scalar.copy(lat[:], ring[3][:]).then_inc(act_rel, 1)
                if not last:
                    act.wait_ge(rms_step, b * 3 + 3)
                    squares(b + 1)
                act.wait_ge(pe_done, b * PEN + (PE0 + NOPEK + 1))
                high(b, K, ring[NOPEK % 3][:])
                act.wait_ge(rot_ready, b * 2 + 1)
                high(b, KR, rot[:, 0, :])
                act.wait_ge(v_out, b * DMA + 1)
                for i in range(2):
                    act.wait_ge(pe_done, b * PEN + (PE0 + VAL0 + i + 1))
                    nc.scalar.copy(vs[:, 4 * i:4 * i + 4, :, 0:MHD].rearrange("p s h m -> p (s h) m"),
                                   ring[(VAL0 + i) % 3][:].rearrange("p (a m) -> p a m", m=MHD)).then_inc(act_rel, 1)
                act.wait_ge(pe_done, b * PEN + (PE0 + NOPEQ + 1))
                high(b, Q, ring[NOPEQ % 3][:])
                if not last:
                    transposed(b + 1)
                act.wait_ge(rot_ready, b * 2 + 2)
                high(b, QR, rot[:, 1, :])

            with act.Fori(0, B - 1) as b:
                batch(b, False)
            batch(B - 1, True)

        @block.vector
        def _(dve):
            dve.sem_inc(dve_rel, 1)
            dve.wait_ge(w_in, 10 * DMA)
            dve.wait_ge(const_ready, 9)
            def by_feature(w):
                return w.rearrange("p (h d) -> p d h", h=MH)
            def columns(w):
                return w.rearrange("p (d h) -> p d h", h=MH)
            for c in range(DC):
                dve.tensor_scalar(columns(w_rk[:, c, :]), by_feature(stage_r[:, c, :]), ln1[:, c:c + 1], None,
                                  ALU.mult).then_inc(w_ready, 1)
                dve.tensor_scalar(w_lat[:, c, :], w_lat[:, c, :], ln1[:, c:c + 1], None, ALU.mult).then_inc(w_ready, 1)
            for i, rows in enumerate((slice(0, LAT), slice(LAT, P), slice(LAT, P))):
                scale = 1.0 if i == 0 else float(MHD) ** -0.5
                dve.tensor_scalar(columns(w_up[rows, i, :]), by_feature(stage[rows, i, :]), scale, None,
                                  ALU.mult).then_inc(w_ready, 1)

            def normalise(b):
                dve.wait_ge(rms_step, b * 3 + 3)
                dve.reciprocal(rn[:], rms[:]).then_inc(rn_step, 1)
                dve.wait_ge(rn_step, b + 1)
                if not (isinstance(b, int) and b == 0):
                    dve.wait_ge(pe_done, (b - 1) * PEN + PE0)
                for s in range(ST):
                    dve.tensor_scalar(xn[:, s, :], xin[:, s, :], rn[:, s:s + 1], None, ALU.mult).then_inc(xn_ready, 1)

            normalise(0)

            def rotate(b, i, use):
                src = ring[use % 3]
                dve.wait_ge(pe_done, b * PEN + (PE0 + use + 1))
                dve.tensor_tensor(t1[:], src[:], cos[:], ALU.mult).then_inc(rope_step, 1)
                dve.tensor_tensor(t2[0:64, :], src[64:P, :], sin[0:64, :], ALU.mult)
                dve.tensor_tensor(t2[64:P, :], src[0:64, :], sin[64:P, :], ALU.mult).then_inc(dve_rel, 1)
                dve.wait_ge(rope_step, b * 2 + (i + 1))
                dve.wait_ge(dve_rel, b * 4 + (2 if i == 0 else 5))
                dve.tensor_tensor(rot[:, i, :], t1[:], t2[:], ALU.add).then_inc(rot_ready, 1)

            def split(b, j, src, rel):
                dve.wait_ge(h_ready, b * 4 + (j + 1))
                dve.wait_ge(part_out[j], b * PARTS + 1)
                dve.tensor_tensor(r1[:, j, :], src, part[:, j, 0, :], ALU.subtract).then_inc(rel, 1)

            def middle(b, j):
                dve.tensor_copy(part[:, j, 1, :], r1[:, j, :]).then_inc(m_ready, 1)

            def batch(b, last):
                rotate(b, 0, ROPEK)
                split(b, K, ring[NOPEK % 3][:], dve_rel)
                dve.wait_ge(dve_rel, b * 4 + 3)
                middle(b, K)
                split(b, KR, rot[:, 0, :], r1_ready)
                dve.wait_ge(r1_ready, b * 2 + 1)
                middle(b, KR)
                if not last:
                    normalise(b + 1)
                split(b, Q, ring[NOPEQ % 3][:], dve_rel)
                dve.wait_ge(dve_rel, b * 4 + 4)
                middle(b, Q)
                rotate(b, 1, ROPEQ)
                split(b, QR, rot[:, 1, :], r1_ready)
                dve.wait_ge(r1_ready, b * 2 + 2)
                middle(b, QR)

            with dve.Fori(0, B - 1) as b:
                batch(b, False)
            batch(B - 1, True)

        @block.tensor
        def _(pe):
            pe.wait_ge(const_ready, 9)

            def transposes(b, first):
                pe.wait_ge(xn_ready, b * ST + ST)
                for i in range(2):
                    if not first:
                        if i == 0:
                            pe.wait_ge(act_rel, (b - 1) * 5 + 5)
                        else:
                            pe.wait_ge(dve_rel, (b - 1) * 4 + 4)
                    for c in range(DC):
                        for s in range(4):
                            at = c * HALF + s * P
                            last = pe.transpose(ring[(TR0 + i) % 3][:, at:at + P], xn[:, 4 * i + s, c * P:(c + 1) * P], ident[:])
                    last.then_inc(pe_done, 1)

            transposes(0, True)
            pe.wait_ge(w_ready, 7)

            def project(use, pairs):
                for h in range(NH):
                    cols = slice(h * HALF, (h + 1) * HALF)
                    for i, (w, src) in enumerate(pairs):
                        last = pe.matmul(ring[3 if use == LATENT else use % 3][:, cols], w, src[:, cols], start=i == 0, stop=i == len(pairs) - 1)
                last.then_inc(pe_done, 1)

            def batch(b, last_batch):
                pe.wait_ge(act_rel, b * 5 + 2)
                project(LATENT, [(w_lat[:, c, :], xT[:, c, :]) for c in range(DC)])
                project(ROPEK, [(w_rk[:, c, :], xT[:, c, :]) for c in range(DC)])
                pe.wait_ge(act_rel, b * 5 + 3)
                project(NOPEK, [(w_up[:, 0, :], lat[:])])
                for i in range(2):
                    if i == 0:
                        pe.wait_ge(dve_rel, b * 4 + 1)
                    if i == 1:
                        pe.wait_ge(dve_rel, b * 4 + 2)
                    for s in range(4):
                        at = (4 * i + s) * P
                        last = pe.matmul(ring[(VAL0 + i) % 3][:, s * D:(s + 1) * D], lat[:, at:at + P], w_v[:],
                                         start=s % 2 == 0, stop=s % 2 == 1, skip_group_check=True)
                    last.then_inc(pe_done, 1)
                pe.wait_ge(dve_rel, b * 4 + 3)
                project(NOPEQ, [(w_up[:, 1, :], lat[:])])
                pe.wait_ge(act_rel, b * 5 + 4)
                project(ROPEQ, [(w_up[:, 2, :], lat[:])])
                if not last_batch:
                    transposes(b + 1, False)

            with pe.Fori(0, B - 1) as b:
                batch(b, False)
            batch(B - 1, True)


def rope_table():
    inv = (1.0 / np.float32(10000.0) ** (np.arange(0, ROPE_W, 2, dtype=np.float32) / np.float32(ROPE_W))).astype(np.float32)
    angle = np.arange(S, dtype=np.float32)[None, :] * np.concatenate([inv, inv])[:, None]
    sign = np.where(np.arange(ROPE_W) < ROPE_W // 2, -1, 1).astype(np.float32)[:, None]
    return np.stack([np.cos(angle), np.sin(angle) * sign]).astype(np.float32)



GH = 4
NG = MH // GH
HI, MID, LO = range(3)
ROWS = QK_ROWS + 3
NEG = -3.0e38
Y_UNITS = [(i, jj, part) for i in range(ST) for part in range(i // 4 + 1) for jj in range(GH // 2)]
Y_STEPS = [(0, i) for i in range(4)] + [(1, i) for i in range(ST)]


def softmax_attention(nc, qp, kp, v_dram, y_dram):
    UN, SN = len(Y_UNITS), len(Y_STEPS)
    EN = SN * GH
    LOAD = 7 * DMA

    def at(b, g, per, n):
        return b * (NG * per) + (g * per + n)

    with ExitStack() as ctx:
        def sb(name, shape, dt=F32):
            return ctx.enter_context(nc.sbuf_tensor("sm_" + name, shape, dt))

        def sem(name):
            return ctx.enter_context(nc.semaphore("sm_" + name))

        qs = [sb(f"qs{i}", [ROWS, GH, S], BF16) for i in range(NG)]
        ks = [sb(f"ks{i}", [ROWS, GH, S], BF16) for i in range(NG)]
        vp = [sb(f"vp{i}", [P, ST, GH * VW]) for i in range(NG)]
        pt = [sb(f"pt{i}", [P, GH, HALF]) for i in range(3)]
        ident = sb("ident3", [P, P], BF16)
        mask = sb("mask", [P, P], BF16)
        mask_t = sb("mask_t", [P, P], BF16)
        zero = sb("zero", [P, GH * ST])
        mx = [sb(f"mx{i}", [P, 2, ST, GH]) for i in range(2)]
        neg = [sb(f"neg{i}", [P, GH * ST]) for i in range(2)]
        rem = [sb(f"rem{i}", [P, GH * ST]) for i in range(2)]
        nb = [sb(f"nb{i}", [P, 3, GH * ST], BF16) for i in range(2)]
        mt = [sb(f"mt{i}", [QK_ROWS, P], BF16) for i in range(2)]
        yb = [sb(f"yb{i}", [P, HALF]) for i in range(2)]
        psA = [ctx.enter_context(nc.psum_tensor(f"sm_psMax{i}", [P, 2, HALF], F32)) for i in range(2)]
        psB = [ctx.enter_context(nc.psum_tensor(f"sm_psS{i}", [P, HALF], F32)) for i in range(3)]
        psO = ctx.enter_context(nc.psum_tensor("psO", [P, HALF], F32))
        psM = psA[0]

        load_in = [sem(f"load_in{i}") for i in range(NG)]
        m_in = sem("m_in")
        y_out = [sem(f"y_out{i}") for i in range(2)]
        const_ready, ones_ready = sem("const3_ready"), sem("ones_ready")
        max_ready, max_used = sem("max_ready"), sem("max_used")
        mx_ready, neg_step = sem("mx_ready"), sem("neg_step")
        mt_ready, mt_copied = sem("mt_ready"), sem("mt_copied")
        s_ready, e_ready = sem("s_ready"), sem("exp_ready")
        y_turn = sem("y_turn")
        pv_done, y_copied = sem("pv_done"), sem("y_copied")

        block = ctx.enter_context(nc.Block())

        @block.sync
        def _(sp):
            for i in range(2):
                sp.sem_inc(y_out[i], 1)

            def load(b, g):
                b, g = (b, g) if g < NG else (b + 1, g - NG)

                def rows(src, part, n, same):
                    f = src[b, part].rearrange("(d h) t -> d h t", h=MH)[:, GH * g:GH * g + GH, :]
                    if n == 1:
                        return f.rearrange("d h t -> d (h t)")
                    if same:
                        return f.rearrange("d h t -> d (h t)").unsqueeze(0).broadcast_to([n, MHD, GH * S])
                    return src[b, part:part + n].rearrange("c (d h) t -> c d h t", h=MH)[:, :, GH * g:GH * g + GH, :]\
                        .rearrange("c d h t -> c d (h t)")

                for dst, src, same in ((qs[g], qp, True), (ks[g], kp, False)):
                    for lo, n, part in ((0, 3, HI), (48, 2, MID if same else HI), (80, 1, LO if same else HI)):
                        sp.dma_start(dst[lo:lo + 16 * n].rearrange("p h t -> p (h t)"),
                                     rows(src, part, n, same)).then_inc(load_in[g], DMA)
                sp.dma_start(vp[g][:], v_dram[b].rearrange("(i t) c -> t i c", t=P)[
                    :, :, g * GH * VW:(g + 1) * GH * VW]).then_inc(load_in[g], DMA)

            def store_maxima(b, g):
                sp.wait_ge(mt_copied, at(b, g, 1, 2))
                dst, src = qs[(g + 1) % NG], mt[(g + 1) % 2]
                for part in range(3):
                    sp.dma_start(dst[QK_ROWS + part:QK_ROWS + part + 1].rearrange("p h (i t) -> p (h i) t", t=P),
                                 src[part * 32:(part + 1) * 32, :]).then_inc(m_in, DMA)

            def store_y(b, g, qh):
                sp.wait_ge(y_copied, at(b, g, 2, qh + 1))
                sp.sem_inc(y_turn, 1)
                sp.dma_start(y_dram[b, qh, g], yb[qh][:]).then_inc(y_out[qh], DMA)

            for g in range(3):
                load(0, g)
            store_maxima(0, -1)

            def group(b, g, last):
                if not (last and g == NG - 1):
                    sp.wait_ge(pv_done, at(b, g, SN, 3))
                if not (last and g > 0):
                    load(b, g + 3)
                store_y(b, g, 0)
                if not (last and g == NG - 1):
                    store_maxima(b, g)
                store_y(b, g, 1)

            with sp.Fori(0, B - 1) as b:
                for g in range(NG):
                    group(b, g, False)
            for g in range(NG):
                group(B - 1, g, True)
            for i in range(2):
                sp.wait_ge(y_out[i], B * NG * DMA + 1)

        @block.gpsimd
        def _(pool):
            pool.memset(zero[:], 0.0).then_inc(const_ready, 1)
            pool.memset(ident[:], 0.0).then_inc(const_ready, 1)
            pool.memset(mask[:], 0.0).then_inc(const_ready, 1)
            pool.memset(mask_t[:], 0.0).then_inc(const_ready, 1)
            pool.wait_ge(const_ready, 4)
            pool.affine_select(out=ident[:], in_=ident[:], compare_op=ALU.not_equal, fill=1.0, base=0,
                               pattern=[[-1, P]], channel_multiplier=1).then_inc(const_ready, 1)
            pool.affine_select(out=mask[:], in_=mask[:], compare_op=ALU.is_ge, fill=NEG, base=0,
                               pattern=[[-1, P]], channel_multiplier=1).then_inc(const_ready, 1)
            pool.affine_select(out=mask_t[:], in_=mask_t[:], compare_op=ALU.is_ge, fill=NEG, base=0,
                               pattern=[[1, P]], channel_multiplier=-1).then_inc(const_ready, 1)

            pool.wait_ge(const_ready, 7)
            for i in range(NG):
                pool.memset(ks[i][QK_ROWS:ROWS], 1.0).then_inc(ones_ready, 1)
                pool.wait_ge(ones_ready, i + 1)

            def negate(b, g, par):
                def done(n):
                    return at(b, g, 5, n)
                pool.wait_ge(mx_ready, at(b, g, 1, 1))
                pool.tensor_tensor(neg[par][:].rearrange("p (j i) -> p j i", j=GH), zero[:].rearrange("p (j i) -> p j i", j=GH),
                                   mx[par][:, 0].rearrange("p i j -> p j i"), ALU.subtract).then_inc(neg_step, 1)
                pool.wait_ge(neg_step, done(1))
                pool.tensor_tensor(nb[par][:, HI], neg[par][:], zero[:], ALU.add).then_inc(neg_step, 1)
                pool.wait_ge(neg_step, done(2))
                pool.tensor_tensor(rem[par][:], neg[par][:], nb[par][:, HI], ALU.subtract).then_inc(neg_step, 1)
                pool.wait_ge(neg_step, done(3))
                pool.tensor_tensor(nb[par][:, MID], rem[par][:], zero[:], ALU.add).then_inc(neg_step, 1)
                pool.wait_ge(neg_step, done(4))
                pool.tensor_tensor(nb[par][:, LO], rem[par][:], nb[par][:, MID], ALU.subtract).then_inc(neg_step, 1)

            negate(0, 0, 0)

            def group(b, g, last):
                if not (last and g == NG - 1):
                    negate(b, g + 1, (g + 1) % 2)

            with pool.Fori(0, B - 1) as b:
                for g in range(NG):
                    group(b, g, False)
            for g in range(NG):
                group(B - 1, g, True)

        @block.vector
        def _(dve):
            dve.sem_inc(max_used, 2)

            def unit(b, g, u):
                g, par = g, g % 2
                i, jj, part = Y_UNITS[u]
                if u == 0 and not (isinstance(b, int) and b == 0 and g < 2):
                    dve.wait_ge(neg_step, at(b, g - 2, 5, 1))
                w = P * (i + 1) - HALF * part if part == i // 4 else HALF
                dve.wait_ge(max_ready, at(b, g, UN, u + 1))
                dve.tensor_reduce(mx[par][:, part, i, 2 * jj:2 * jj + 2], psA[u % 2][:, :, 0:w],
                                  AX.X, ALU.max).then_inc(max_used, 1)
                if u == UN - 1:
                    dve.wait_ge(max_used, at(b, g, UN, UN + 2))
                    dve.tensor_tensor(mx[par][:, 0, 4:ST], mx[par][:, 0, 4:ST], mx[par][:, 1, 4:ST],
                                      ALU.max).then_inc(mx_ready, 1)

            for u in range(UN):
                unit(0, 0, u)
            for u in range(UN // 2):
                unit(0, 1, u)

            def group(b, g, last):
                for k in range(SN):
                    ahead, us = (1, (12 + 2 * k, 13 + 2 * k)) if k < 6 else (2, (2 * k - 12, 2 * k - 11))
                    if not (last and g + ahead >= NG):
                        for u in us:
                            unit(b, g + ahead, u)

            with dve.Fori(0, B - 1) as b:
                for g in range(NG):
                    group(b, g, False)
            for g in range(NG):
                group(B - 1, g, True)

        @block.scalar
        def _(act):
            act.sem_inc(e_ready, 3)

            def copy_maxima(b, g):
                par = (g + 1) % 2
                act.wait_ge(mt_ready, at(b, g, 1, 2))
                nc.scalar.copy(mt[par][:], psM[0:QK_ROWS, 0, 0:P]).then_inc(mt_copied, 1)

            def copy_y(b, g, qh):
                act.wait_ge(pv_done, at(b, g, SN, (SN if qh else 4) + 3))
                act.wait_ge(y_out[qh], at(b, g, DMA, 1))
                nc.scalar.copy(yb[qh][:], psO[:]).then_inc(y_copied, 1)

            copy_maxima(0, -1)

            def group(b, g, first, last):
                for k, (qh, i) in enumerate(Y_STEPS):
                    q0 = max(HALF * qh, P * i)
                    n = HALF * (qh + 1) - q0
                    if k == 9 and not (last and g == NG - 1):
                        copy_maxima(b, g)
                    for j in range(GH):
                        act.wait_ge(s_ready, at(b, g, EN, k * GH + j + 1))
                        if j == 0:
                            act.wait_ge(pv_done, at(b, g, SN, k + 1))
                        nc.scalar.activation(pt[k % 3][:, j, 0:n], psB[(k * GH + j) % 3][:, 0:n], ACT.Exp).then_inc(e_ready, 1)
                        if j == 1 and k == 1 and not (first and g == 0):
                            copy_y(b, g - 1, 1)
                        if j == 1 and k == 5:
                            copy_y(b, g, 0)

            for g in range(NG):
                group(0, g, True, False)
            with act.Fori(1, B - 1) as b:
                for g in range(NG):
                    group(b, g, False, False)
            for g in range(NG):
                group(B - 1, g, False, True)
            copy_y(B - 1, NG - 1, 1)

        @block.tensor
        def _(pe):
            pe.sem_inc(pv_done, 3)
            pe.wait_ge(const_ready, 7)

            def unit(b, g, u):
                i, jj, part = Y_UNITS[u]
                if u == 0:
                    over = g // NG
                    pe.wait_ge(load_in[g % NG], (b + over) * LOAD + LOAD)
                diagonal = part == i // 4
                w = P * (i + 1) - HALF * part if diagonal else HALF
                q, kk = qs[g % NG], ks[g % NG]
                pe.wait_ge(max_used, at(b, g, UN, u + 1))
                if u == 6 and not (isinstance(b, int) and b == 0 and g == 0):
                    pe.wait_ge(mt_copied, at(b, g - 2, 1, 2))
                for a in range(2):
                    j = 2 * jj + a
                    last = pe.matmul(psA[u % 2][:, a, 0:w], q[0:QK_ROWS, j, i * P:(i + 1) * P],
                                     kk[0:QK_ROWS, j, part * HALF:part * HALF + w], start=True, stop=not diagonal)
                    if diagonal:
                        last = pe.matmul(psA[u % 2][:, a, w - P:w], ident[:], mask[:], start=False, stop=True)
                last.then_inc(max_ready, 1)

            def transpose_maxima(b, g, last=False):
                par = (g + 1) % 2
                pe.wait_ge(neg_step, at(b, g, 5, 10))
                if not (isinstance(b, int) and b == 0 and g == -1):
                    pe.wait_ge(mt_copied, at(b, g, 1, 1))
                if g < 0:
                    pe.wait_ge(max_used, at(b, 1, UN, 7))
                elif last and g + 2 >= NG:
                    pe.wait_ge(max_used, at(b, NG - 1, UN, UN + 1))
                else:
                    pe.wait_ge(max_used, at(b, g + 2, UN, 7))
                pe.matmul(psM[0:QK_ROWS, 0, 0:P], nb[par][:].rearrange("p c n -> p (c n)"), ident[:],
                          start=True, stop=True).then_inc(mt_ready, 1)

            for u in range(UN):
                unit(0, 0, u)
            for u in range(UN // 2):
                if u == 6:
                    transpose_maxima(0, -1)
                unit(0, 1, u)
            pe.wait_ge(ones_ready, NG)

            def weighted_sum(b, g, k):
                qh, i = Y_STEPS[k]
                q0 = max(HALF * qh, P * i)
                n = HALF * (qh + 1) - q0
                pe.wait_ge(e_ready, at(b, g, EN, (k + 1) * GH + 3))
                if i == 0 and not (isinstance(b, int) and b == 0 and g == 0 and qh == 0):
                    pe.wait_ge(y_copied, at(b, g, 2, qh))
                for j in range(GH):
                    last = pe.matmul(psO[VW * j:VW * (j + 1), q0 - HALF * qh:HALF], vp[g % NG][:, i, VW * j:VW * (j + 1)],
                                     pt[k % 3][:, j, 0:n], start=i == 0, stop=i == 4 * qh + 3)
                last.then_inc(pv_done, 1)

            def group(b, g, first, last):
                for k, (qh, i) in enumerate(Y_STEPS):
                    q0 = max(HALF * qh, P * i)
                    n = HALF * (qh + 1) - q0
                    if k == 0:
                        pe.wait_ge(m_in, at(b, g, 3 * DMA, 3 * DMA))
                    ahead, us = (1, (12 + 2 * k, 13 + 2 * k)) if k < 6 else (2, (2 * k - 12, 2 * k - 11))
                    for j in range(GH):
                        pe.wait_ge(e_ready, at(b, g, EN, k * GH + j + 1))
                        diagonal = i // 4 == qh
                        done = pe.matmul(psB[(k * GH + j) % 3][:, 0:n], ks[g][:, j, i * P:(i + 1) * P], qs[g][:, j, q0:q0 + n],
                                         start=True, stop=not diagonal)
                        if diagonal:
                            done = pe.matmul(psB[(k * GH + j) % 3][:, 0:P], ident[:], mask_t[:], start=False, stop=True)
                        done.then_inc(s_ready, 1)
                        if j % 2 == 1 and not (last and g + ahead >= NG):
                            unit(b, g + ahead, us[j // 2])
                    if k == 9 - 1 and not (last and g == NG - 1):
                        transpose_maxima(b, g, last)
                    if k >= 1:
                        weighted_sum(b, g, k - 1)
                    elif not (first and g == 0):
                        weighted_sum(b if g > 0 else b - 1, g - 1 if g > 0 else NG - 1, SN - 1)

            for g in range(NG):
                group(0, g, True, False)
            with pe.Fori(1, B - 1) as b:
                for g in range(NG):
                    group(b, g, False, False)
            for g in range(NG):
                group(B - 1, g, False, True)
            weighted_sum(B - 1, NG - 1, SN - 1)



NBLK = B * NH
TT = HALF // P
ER = 7
ROUTER_STEPS = 18
NE = ER + 1
WGT, WUP, WDN = range(3)


def output_and_router(nc, y_dram, x1, W_o, w_ln2, W_router, routing_bias,
                      Wg_s, Wu_s, Wd_s, Wg_r, Wu_r, Wd_r, x12, xT2, wt_rows, w_hi, w_lo, x_hi, x_lo):
    with ExitStack() as ctx:
        def sb(name, shape, dt=F32):
            return ctx.enter_context(nc.sbuf_tensor("rt_" + name, shape, dt))

        def ps(name):
            return ctx.enter_context(nc.psum_tensor("rt_" + name, [P, HALF], F32))

        def sem(name):
            return ctx.enter_context(nc.semaphore("rt_" + name))

        ident = sb("ident4", [P, P])
        wo = sb("wo4", [P, DC, D])
        wr = sb("wr", [P, DC, ER])
        ln2 = sb("ln2", [P, DC])
        rb = sb("rb", [P, ER])
        rank = sb("rank", [P, NBLK * TT, ER])
        half, inv_d, eps = sb("half4", [P, TT]), sb("inv_d4", [P, TT]), sb("eps4", [P, TT])
        yT = sb("yT", [P, NG, HALF])
        x1b = sb("x1b", [P, TT, D])
        rden = sb("rden", [P, TT, MH])
        yn = sb("yn", [P, TT, D])
        ynT = sb("ynT", [P, DC, HALF])
        x2s, x12s, xn = (sb(n, [P, TT, D]) for n in ("x2s", "x12s", "xn4"))
        ssq, rms, rn = sb("ssq4", [P, TT]), sb("rms4", [P, TT]), sb("rn4", [P, TT])
        xnT = sb("xnT4", [P, DC, HALF])
        w_raw = sb("w_raw", [P, 3, NE, DC, D])
        wts = sb("wts", [P, NBLK * TT, ER])
        wT = yT[0:TT * ER, 0:2, :].rearrange("r g (a p) -> r (g a) p", p=P)
        logit = sb("logit", [P, NBLK * TT, ER])
        prob, tie, hot1, hot2 = (sb(n, [P, NBLK * TT, ER]) for n in ("prob", "tie", "hot1", "hot2"))
        top1, top2, pick, total = (sb(n, [P, NBLK * TT]) for n in ("top1", "top2", "pick", "total"))
        psY, psT, psW = ([ps(f"{n}{i}") for i in range(2)] for n in ("psY", "psT4", "psW"))
        psL = ps("psL")

        w_in, y_in, x1_in = sem("w4_in"), sem("y_in"), sem("x1b_in")
        x12_out, xT_out = sem("x12_out"), sem("xT_out")
        const_ready = sem("const4_ready")
        y_ready, y_used, t_ready, t_used = sem("yT_ready"), sem("yT_used"), sem("t4_ready"), sem("t4_used")
        den_ready = sem("den_ready")
        o_ready, x2_ready, sq_ready = sem("o4_ready"), sem("x2_ready"), sem("sq4_ready")
        rms_step, rn_ready, xn_ready = sem("rms4_step"), sem("rn4_ready"), sem("xn4_ready")
        sum_ready = sem("sum_ready")
        shared_in, routed_in = sem("shared_in"), sem("routed_in")
        split_step, wt_turned, wt_copied, wt_out, xp_step = (sem(n) for n in (
            "split_step", "wt_turned", "wt_copied", "wt_out", "x_parts_step"))
        l_ready, l_used, chain = sem("l4_ready"), sem("l4_used"), sem("router_step")
        p_ready, turn = sem("prob_ready"), sem("turn4")

        block = ctx.enter_context(nc.Block())

        def rows(t_dram, t):
            return t_dram.rearrange("b (h s p) d -> (b h) p s d", h=NH, p=P)[t]

        @block.sync
        def _(sp):
            sp.dma_start(yT[:], y_dram.rearrange("b h g p t -> (b h) p g t")[0]).then_inc(y_in, DMA)
            sp.dma_start(x1b[:], rows(x1, 0)).then_inc(x1_in, DMA)
            sp.dma_start(wo[:], W_o.rearrange("(c p) n -> p c n", p=P)).then_inc(w_in, DMA)
            sp.dma_start(wr[:], W_router.rearrange("(c p) n -> p c n", p=P)).then_inc(w_in, DMA)
            sp.dma_start(ln2[:], w_ln2.rearrange("(c p) -> p c", p=P), allow_slow_non_contiguous=True).then_inc(w_in, DMA)
            sp.dma_start(rb[:], routing_bias.partition_broadcast(P)).then_inc(w_in, DMA)
            for j, w in enumerate((Wg_s, Wu_s, Wd_s)):
                sp.dma_start(w_raw[:, j, 0], w.rearrange("(c p) n -> p c n", p=P)).then_inc(shared_in, DMA)
            sp.sem_inc(x12_out, 1)
            sp.sem_inc(xT_out, 1)

            def load_y(t):
                sp.wait_ge(y_ready, t * TT)
                sp.sem_inc(turn, 1)
                sp.dma_start(yT[:], y_dram.rearrange("b h g p t -> (b h) p g t")[t]).then_inc(y_in, DMA)

            def body(t, last):
                if not last:
                    sp.wait_ge(sum_ready, t + 1)
                    sp.sem_inc(turn, 1)
                    sp.dma_start(x1b[:], rows(x1, t + 1)).then_inc(x1_in, DMA)
                sp.wait_ge(sum_ready, t + 1)
                sp.sem_inc(turn, 1)
                sp.dma_start(rows(x12, t), x12s[:]).then_inc(x12_out, DMA)
                sp.wait_ge(t_used, t * 4 + (4 if last else 6))
                sp.sem_inc(turn, 1)
                sp.dma_start(xT2[t], xnT[:]).then_inc(xT_out, DMA)

            load_y(1)
            for j, w in enumerate((Wg_r, Wu_r, Wd_r)):
                if j > 0:
                    load_y(j + 1)
                sp.dma_start(w_raw[:, j, 1:NE], w.rearrange("e (c p) n -> p e c n", p=P)).then_inc(routed_in, DMA)
                if j > 0:
                    body(j - 1, False)
            with sp.Fori(2, NBLK - 2) as t:
                load_y(t + 2)
                body(t, False)
            body(NBLK - 2, False)
            body(NBLK - 1, True)
            sp.wait_ge(wt_copied, 2)
            for s in range(TT):
                sp.dma_start(wt_rows[:, :, s * P:(s + 1) * P].rearrange("t e p -> e t p"),
                             wT[ER * s:ER * s + ER]).then_inc(wt_out, DMA)
            sp.wait_ge(wt_out, TT * DMA)
            sp.wait_ge(x12_out, NBLK * DMA + 1)
            sp.wait_ge(xT_out, NBLK * DMA + 1)

        @block.gpsimd
        def _(pool):
            pool.memset(ident[:], 0.0).then_inc(const_ready, 1)
            pool.memset(half[:], 0.5).then_inc(const_ready, 1)
            pool.memset(inv_d[:], 1.0 / D).then_inc(const_ready, 1)
            pool.memset(eps[:], RMS_EPS).then_inc(const_ready, 1)
            for e in range(ER):
                pool.memset(rank[:, :, e], float(ER - e)).then_inc(const_ready, 1)
            pool.wait_ge(const_ready, 4 + ER)
            pool.affine_select(out=ident[:], in_=ident[:], compare_op=ALU.not_equal, fill=1.0, base=0,
                               pattern=[[-1, P]], channel_multiplier=1).then_inc(const_ready, 1)

            def split(e):
                raw, hi, lo = (w.rearrange("p j c n -> p j (c n)") for w in (w_raw[:, :, e], w_hi[:, e], w_lo[:, e]))
                pool.wait_ge(shared_in if e == 0 else routed_in, 3 * DMA)
                pool.tensor_copy(hi, raw).then_inc(split_step, 1)
                pool.wait_ge(split_step, 2 * e + 1)
                pool.tensor_tensor(lo, raw, hi, ALU.subtract).then_inc(split_step, 1)

            for t in range(NBLK):
                pool.wait_ge(sq_ready, t * TT + TT)
                pool.tensor_tensor(rms[:], ssq[:], inv_d[:], ALU.mult).then_inc(rms_step, 1)
                pool.wait_ge(rms_step, t * 3 + 1)
                pool.tensor_tensor(rms[:], rms[:], half[:], ALU.pow).then_inc(rms_step, 1)
                pool.wait_ge(rms_step, t * 3 + 2)
                pool.tensor_tensor(rms[:], rms[:], eps[:], ALU.add).then_inc(rms_step, 1)
                if t == 0:
                    split(0)
                elif t >= 2:
                    split(t - 1)
            split(NE - 1)

        @block.scalar
        def _(act):
            def first(t, seen):
                for i in range(2):
                    act.wait_ge(t_ready, seen + (i + 1))
                    nc.scalar.copy(ynT[:, :, i * 256:(i + 1) * 256], psT[i][:].rearrange("p (c n) -> p c n", c=DC)).then_inc(t_used, 1)

            def squares(t):
                for s in range(TT):
                    act.wait_ge(x2_ready, t * TT + (s + 1))
                    nc.scalar.activation(xn[:, s, :], x2s[:, s, :], ACT.Square, accum_out=ssq[:, s:s + 1]).then_inc(sq_ready, 1)

            def second(t, seen):
                act.wait_ge(xT_out, t * DMA + 1)
                for i in range(2):
                    act.wait_ge(t_ready, seen + (i + 1))
                    for c in range(DC):
                        last = nc.scalar.activation(xnT[:, c, i * 256:(i + 1) * 256], psT[i][:, c * 256:(c + 1) * 256],
                                                    ACT.Copy, scale=ln2[:, c:c + 1])
                    last.then_inc(t_used, 1)

            first(0, 0)

            def body(t, last):
                squares(t)
                if not last:
                    first(t + 1, t * 4 + 2)
                second(t, t * 4 + (2 if last else 4))

            body(0, False)
            act.wait_ge(xp_step, 2)
            with act.Fori(1, NBLK - 1) as t:
                body(t, False)
            body(NBLK - 1, True)
            act.wait_ge(l_used, NBLK)
            nc.scalar.activation(prob[:], logit[:], ACT.Sigmoid).then_inc(p_ready, 1)
            for i in range(2):
                act.wait_ge(wt_turned, i + 1)
                nc.scalar.copy(wT[:, 4 * i:4 * i + 4], psT[i][0:TT * ER, :].rearrange("p (t n) -> p t n", n=P)).then_inc(wt_copied, 1)

        @block.vector
        def _(dve):
            dve.wait_ge(w_in, 4 * DMA)
            dve.wait_ge(const_ready, 5 + ER)

            def first(t):
                for s in range(TT):
                    src = psY[s % 2][:].rearrange("p (h m) -> p h m", m=VW)
                    dve.wait_ge(y_ready, t * TT + (s + 1))
                    dve.reciprocal(rden[:, s, :], src[:, :, MHD]).then_inc(den_ready, 1)
                    dve.wait_ge(den_ready, t * TT + (s + 1))
                    dve.tensor_tensor(yn[:, s, :].rearrange("p (h m) -> p h m", m=MHD), src[:, :, 0:MHD],
                                      rden[:, s, :].unsqueeze(2).broadcast_to([P, MH, MHD]), ALU.mult).then_inc(y_used, 1)

            def second(t):
                dve.wait_ge(x1_in, t * DMA + DMA)
                for s in range(TT):
                    dve.wait_ge(o_ready, t * 2 + (s // 2 + 1))
                    dve.tensor_tensor(x2s[:, s, :], psW[s // 2][:, (s % 2) * D:(s % 2 + 1) * D], x1b[:, s, :],
                                      ALU.add).then_inc(x2_ready, 1)

            def sum_x(t):
                dve.wait_ge(x12_out, t * DMA + 1)
                dve.wait_ge(x2_ready, t * TT + TT)
                dve.tensor_tensor(x12s[:], x2s[:], x1b[:], ALU.add).then_inc(sum_ready, 1)

            def norm(t):
                dve.wait_ge(rms_step, t * 3 + 3)
                dve.reciprocal(rn[:], rms[:]).then_inc(rn_ready, 1)
                dve.wait_ge(rn_ready, t + 1)
                for s in range(TT):
                    dve.tensor_scalar(xn[:, s, :], x2s[:, s, :], rn[:, s:s + 1], None, ALU.mult).then_inc(xn_ready, 1)

            def logits(t):
                dve.wait_ge(l_ready, t + 1)
                dve.tensor_tensor(logit[:, bass.ts(t, TT), :], psL[:, 0:8 * TT].rearrange("p (s e) -> p s e", e=8)[:, :, 0:ER],
                                  rb[:].unsqueeze(1).broadcast_to([P, TT, ER]), ALU.add).then_inc(l_used, 1)

            def body(t, start, last):
                second(t)
                if not last:
                    first(t + 1)
                sum_x(t)
                if not start:
                    logits(t - 1)
                norm(t)

            first(0)
            body(0, True, False)
            dve.wait_ge(t_used, 6)
            dve.tensor_copy(x_hi[0][:], xnT[:]).then_inc(xp_step, 1)
            dve.wait_ge(xp_step, 1)
            dve.tensor_tensor(x_lo[0][:], xnT[:], x_hi[0][:], ALU.subtract).then_inc(xp_step, 1)
            with dve.Fori(1, NBLK - 1) as t:
                body(t, False, False)
            body(NBLK - 1, False, True)
            logits(NBLK - 1)

            steps = [0]

            def then(ins):
                steps[0] += 1
                ins.then_inc(chain, 1)
                dve.wait_ge(chain, steps[0])

            def wide(v):
                return v[:].unsqueeze(2).broadcast_to([P, NBLK * TT, ER])

            dve.wait_ge(p_ready, 1)
            for top, hot in ((top1, hot1), (top2, hot2)):
                then(dve.tensor_reduce(top[:], prob[:], AX.X, ALU.max))
                then(dve.tensor_tensor(tie[:], prob[:], wide(top), ALU.is_equal))
                then(dve.tensor_tensor(tie[:], tie[:], rank[:], ALU.mult))
                then(dve.tensor_reduce(pick[:], tie[:], AX.X, ALU.max))
                then(dve.tensor_tensor(hot[:], tie[:], wide(pick), ALU.is_equal))
                if hot is hot1:
                    then(dve.scalar_tensor_tensor(prob[:], hot[:], -2.0, prob[:], ALU.mult, ALU.add))
            then(dve.tensor_tensor(total[:], top1[:], top2[:], ALU.add))
            then(dve.reciprocal(total[:], total[:]))
            then(dve.tensor_tensor(top1[:], top1[:], total[:], ALU.mult))
            then(dve.tensor_tensor(top2[:], top2[:], total[:], ALU.mult))
            then(dve.tensor_tensor(hot1[:], hot1[:], wide(top1), ALU.mult))
            then(dve.tensor_tensor(hot2[:], hot2[:], wide(top2), ALU.mult))
            then(dve.tensor_tensor(wts[:], hot1[:], hot2[:], ALU.add))

        @block.tensor
        def _(pe):
            pe.wait_ge(const_ready, 5 + ER)

            def turn(dst, src):
                for c in range(DC):
                    for a in range(2):
                        at = c * 256 + a * P
                        last = pe.transpose(dst[:, at:at + P], src[:, a, c * P:(c + 1) * P], ident[:])
                last.then_inc(t_ready, 1)

            def outputs(t):
                pe.wait_ge(y_in, t * DMA + DMA)
                for s in range(TT):
                    if not (isinstance(t, int) and s < 2):
                        pe.wait_ge(y_used, t * TT + (s - 1))
                    for g in range(NG):
                        last = pe.transpose(psY[s % 2][:, g * P:(g + 1) * P], yT[:, g, s * P:(s + 1) * P], ident[:])
                    last.then_inc(y_ready, 1)
                for i in range(2):
                    pe.wait_ge(y_used, t * TT + 2 * (i + 1))
                    if not isinstance(t, int):
                        pe.wait_ge(t_used, t * 4 + (i - 3))
                    turn(psT[i], yn[:, 2 * i:2 * i + 2, :])

            def router(t, last):
                pe.wait_ge(t_used, t * 4 + (4 if last else 6))
                for s in range(TT):
                    for c in range(DC):
                        mm = pe.matmul(psL[:, 8 * s:8 * s + ER], xnT[:, c, s * P:(s + 1) * P], wr[:, c, :],
                                       start=c == 0, stop=c == DC - 1)
                mm.then_inc(l_ready, 1)

            def body(t, start, last):
                for i in range(2):
                    pe.wait_ge(t_used, t * 4 + (i + 1) if isinstance(t, int) and t == 0 else t * 4 + (i - 1))
                    for a in range(2):
                        s = 2 * i + a
                        for c in range(DC):
                            mm = pe.matmul(psW[i][:, a * D:(a + 1) * D], ynT[:, c, s * P:(s + 1) * P], wo[:, c, :],
                                           start=c == 0, stop=c == DC - 1)
                    mm.then_inc(o_ready, 1)
                if not last:
                    outputs(t + 1)
                if not start:
                    router(t - 1, False)
                for i in range(2):
                    pe.wait_ge(xn_ready, t * TT + 2 * (i + 1))
                    if not last:
                        pe.wait_ge(t_used, t * 4 + (i + 3))
                    turn(psT[i], xn[:, 2 * i:2 * i + 2, :])

            outputs(0)
            pe.wait_ge(w_in, 4 * DMA)
            body(0, True, False)
            with pe.Fori(1, NBLK - 1) as t:
                body(t, False, False)
            body(NBLK - 1, False, True)
            router(NBLK - 1, True)

            pe.wait_ge(chain, ROUTER_STEPS)
            for i in range(2):
                for k in range(4):
                    t = 4 * i + k
                    last = pe.transpose(psT[i][0:TT * ER, k * P:(k + 1) * P],
                                        wts[:, t * TT:(t + 1) * TT, :].rearrange("p s e -> p (s e)"), ident[:])
                last.then_inc(wt_turned, 1)


def experts(nc, x12, xT2, wt_rows, w_hi, w_lo, x_hi, x_lo, out):
    NP = DC * NE
    with ExitStack() as ctx:
        def sb(name, shape, dt=F32):
            return ctx.enter_context(nc.sbuf_tensor("ex_" + name, shape, dt))

        def ps(name):
            return ctx.enter_context(nc.psum_tensor("ex_" + name, [P, HALF], F32))

        def sem(name):
            return ctx.enter_context(nc.semaphore("ex_" + name))

        ident = sb("ident", [P, P])
        eps, mhalf, zero = sb("eps", [P, TT]), sb("mhalf", [P, TT]), sb("zero", [P, DC, HALF])
        xT = [sb(f"xT{i}", [P, DC, HALF]) for i in range(2)]
        wb = [sb(f"wb{i}", [P, ER, HALF]) for i in range(2)]
        acc = [sb(f"acc{i}", [P, TT, D]) for i in range(2)]
        sg, su, hf = sb("silu", [P, 2, HALF]), sb("silu_up", [P, 2, HALF]), sb("hidden", [P, 2, HALF])
        h_hi, h_lo = ([sb(f"{n}{i}", [P, DC, HALF], F32R) for i in range(2)] for n in ("h_hi", "h_lo"))
        dT = sb("down_T", [P, DC, HALF])
        bst, mv = sb("bst", [P, TT, 6]), sb("mv", [P, TT, 2])
        ve, rstd = sb("ve", [P, TT]), sb("rstd", [P, TT])
        psG, psU = ([ps(f"{n}{i}") for i in range(2)] for n in ("psG", "psU"))
        psD = [ps(f"psD{i}") for i in range(DC)]
        psR = [ps(f"psR{i}") for i in range(2)]

        turn = sem("turn")
        x_in, wb_in, a_in = ([sem(f"{n}_in{i}") for i in range(2)] for n in ("xT", "wb", "acc"))
        out_done = [sem(f"out_done{i}") for i in range(2)]
        const_ready, x_step = sem("const_ready"), sem("x_split_step")
        gu_ready, sg_ready, su_ready, hf_ready = (sem(n) for n in ("gu_ready", "silu_ready", "silu_up_ready", "hidden_ready"))
        hi_ready, lo_ready, d_ready = sem("hi_ready"), sem("lo_ready"), sem("down_ready")
        d_copied, r_ready, acc_ready = sem("down_copied"), sem("rows_ready"), sem("acc_ready")
        st_step, mv_ready, rs_step, rs_ready, o_ready = (sem(n) for n in (
            "st_step", "mv_ready", "rs_step", "rs_ready", "ln_ready"))

        block = ctx.enter_context(nc.Block())

        def rows(t_dram, b, q):
            return t_dram[b].rearrange("(h s p) d -> h p s d", h=NH, p=P)[q]

        def before(b, q):
            return (b, 0) if q else (b - 1, 1)

        @block.sync
        def _(sp):
            sp.dma_start(xT[1][:], xT2[1]).then_inc(x_in[1], DMA)
            sp.dma_start(xT[0][:], xT2[NH]).then_inc(x_in[0], DMA)
            for q in range(NH):
                sp.dma_start(wb[q][:], wt_rows[q].partition_broadcast(P)).then_inc(wb_in[q], DMA)
                sp.dma_start(acc[q][:], rows(x12, 0, q)).then_inc(a_in[q], DMA)

            def store(b, q):
                sp.wait_ge(o_ready, b * NH + (q + 1))
                sp.sem_inc(turn, 1)
                sp.dma_start(rows(out, b, q), acc[q][:]).then_inc(out_done[q], DMA)

            def body(b, first, last):
                for q in range(NH):
                    if not (first and q == 0):
                        bb, qq = before(b, q)
                        store(bb, qq)
                        if not (last and q == 1):
                            sp.wait_ge(out_done[qq], bb * DMA + DMA)
                            sp.sem_inc(turn, 1)
                            sp.dma_start(acc[qq][:], rows(x12, bb + 1, qq)).then_inc(a_in[qq], DMA)
                            sp.dma_start(wb[qq][:], wt_rows[bb * NH + (qq + NH)].partition_broadcast(P)).then_inc(wb_in[qq], DMA)
                    if not last and not (first and q == 0):
                        sp.wait_ge(x_step, b * (2 * NH) + 2 * q)
                        sp.sem_inc(turn, 1)
                        sp.dma_start(xT[q][:], xT2[b * NH + (q + NH)]).then_inc(x_in[q], DMA)

            body(0, True, False)
            with sp.Fori(1, B - 1) as b:
                body(b, False, False)
            body(B - 1, False, True)
            store(B - 1, 1)
            for q in range(NH):
                sp.wait_ge(out_done[q], B * DMA)

        @block.gpsimd
        def _(pool):
            pool.memset(ident[:], 0.0).then_inc(const_ready, 1)
            pool.memset(eps[:], LN_EPS).then_inc(const_ready, 1)
            pool.memset(mhalf[:], -0.5).then_inc(const_ready, 1)
            pool.memset(zero[:], 0.0).then_inc(const_ready, 1)
            pool.wait_ge(const_ready, 4)
            pool.affine_select(out=ident[:], in_=ident[:], compare_op=ALU.not_equal, fill=1.0, base=0,
                               pattern=[[-1, P]], channel_multiplier=1).then_inc(const_ready, 1)

            def split(b, q, first):
                pool.wait_ge(x_in[q], b * DMA + q * DMA)
                if not first:
                    pool.wait_ge(gu_ready, b * (NH * NP) + (q * NP - NP))
                pool.tensor_tensor(x_hi[q][:], xT[q][:], zero[:], ALU.add).then_inc(x_step, 1)
                pool.wait_ge(x_step, b * (2 * NH) + (2 * q - 1))
                pool.tensor_tensor(x_lo[q][:], xT[q][:], x_hi[q][:], ALU.subtract).then_inc(x_step, 1)

            def norm(b, q):
                pool.wait_ge(mv_ready, b * (NH * TT) + (q * TT + TT))
                pool.tensor_tensor(ve[:], mv[:, :, 1], eps[:], ALU.add).then_inc(rs_step, 1)
                pool.wait_ge(rs_step, b * NH + (q + 1))
                pool.tensor_tensor(rstd[:], ve[:], mhalf[:], ALU.pow).then_inc(rs_ready, 1)

            def body(b, first, last):
                for q in range(NH):
                    if not (first and q == 0):
                        norm(*before(b, q))
                    if q == 0:
                        split(b, 1, first)
                    elif not last:
                        split(b + 1, 0, False)

            body(0, True, False)
            with pool.Fori(1, B - 1) as b:
                body(b, False, False)
            body(B - 1, False, True)
            norm(B - 1, 1)

        @block.scalar
        def _(act):
            def silu(b, n):
                act.wait_ge(gu_ready, b * (NH * NP) + (n + 1))
                nc.scalar.activation(sg[:, n % 2, :], psG[n % 2][:], ACT.Silu).then_inc(sg_ready, 1)

            def high(b, n):
                act.wait_ge(hf_ready, b * (NH * NP) + (n + 1))
                if not (isinstance(b, int) and b == 0 and n < 2 * DC):
                    act.wait_ge(d_ready, b * (NH * NE) + (n // DC - 1))
                nc.scalar.copy(h_hi[n // DC % 2][:, n % DC, :], hf[:, n % 2, :]).then_inc(hi_ready, 1)

            def copy_down(b, q):
                act.wait_ge(d_ready, b * (NH * NE) + (q * NE + NE))
                for c in range(DC):
                    nc.scalar.copy(dT[:, c, :], psD[c][:]).then_inc(d_copied, 1)

            def body(b, first):
                for n in range(NH * NP):
                    if n > 0:
                        high(b, n - 1)
                    elif not first:
                        high(b - 1, NH * NP - 1)
                    silu(b, n)
                    if n % NP == 1 and not (first and n == 1):
                        copy_down(*before(b, n // NP))

            body(0, True)
            with act.Fori(1, B) as b:
                body(b, False)
            high(B - 1, NH * NP - 1)
            copy_down(B - 1, 1)

        @block.vector
        def _(dve):
            def hidden(b, n):
                q, e = n // NP, n // DC % NE
                start = isinstance(b, int) and b == 0 and n < 2
                dve.wait_ge(sg_ready, b * (NH * NP) + (n + 1))
                if e == 0:
                    if not start:
                        dve.wait_ge(lo_ready, b * (NH * NP) + (n - 1))
                    dve.tensor_tensor(hf[:, n % 2, :], sg[:, n % 2, :], psU[n % 2][:], ALU.mult).then_inc(hf_ready, 1)
                    return
                k = q * (NP - DC) + (n % NP) - DC
                dve.tensor_tensor(su[:, n % 2, :], sg[:, n % 2, :], psU[n % 2][:], ALU.mult).then_inc(su_ready, 1)
                if n % NP == DC:
                    dve.wait_ge(wb_in[q], b * DMA + DMA)
                dve.wait_ge(lo_ready, b * (NH * NP) + (n - 1))
                dve.wait_ge(su_ready, b * (NH * (NP - DC)) + (k + 1))
                dve.tensor_tensor(hf[:, n % 2, :], su[:, n % 2, :], wb[q][:, e - 1, :], ALU.mult).then_inc(hf_ready, 1)

            def low(b, n):
                dve.wait_ge(hi_ready, b * (NH * NP) + (n + 1))
                i = n // DC % 2
                dve.tensor_tensor(h_lo[i][:, n % DC, :], hf[:, n % 2, :], h_hi[i][:, n % DC, :],
                                  ALU.subtract).then_inc(lo_ready, 1)

            def gather(b, q):
                dve.wait_ge(a_in[q], b * DMA + DMA)
                for i in range(2):
                    dve.wait_ge(r_ready, b * (2 * NH) + (2 * q + i + 1))
                    dve.tensor_tensor(acc[q][:, 2 * i:2 * i + 2, :].rearrange("p s d -> p (s d)"), psR[i][:],
                                      acc[q][:, 2 * i:2 * i + 2, :].rearrange("p s d -> p (s d)"), ALU.add).then_inc(acc_ready, 1)
                dve.wait_ge(acc_ready, b * (2 * NH) + (2 * q + 2))
                for s in range(TT):
                    dve.bn_stats(bst[:, s, :], acc[q][:, s, :]).then_inc(st_step, 1)

            def aggregate(b, q):
                dve.wait_ge(st_step, b * (NH * TT) + (q * TT + TT))
                dve.sem_inc(turn, 1)
                for s in range(TT):
                    dve.bn_aggr(mv[:, s, :], bst[:, s, :]).then_inc(mv_ready, 1)

            def normalise(b, q):
                dve.wait_ge(rs_ready, b * NH + (q + 1))
                for s in range(TT):
                    last = dve.tensor_scalar(acc[q][:, s, :], acc[q][:, s, :], mv[:, s, 0:1], rstd[:, s:s + 1],
                                             ALU.subtract, ALU.mult)
                last.then_inc(o_ready, 1)

            def body(b, first):
                for n in range(NH * NP):
                    if n > 0:
                        low(b, n - 1)
                    elif not first:
                        low(b - 1, NH * NP - 1)
                    hidden(b, n)
                    if not (first and n < NP):
                        for at, what in ((3, gather), (5, aggregate), (7, normalise)):
                            if n % NP == at:
                                what(*before(b, n // NP))

            body(0, True)
            with dve.Fori(1, B) as b:
                body(b, False)
            low(B - 1, NH * NP - 1)
            gather(B - 1, 1)
            aggregate(B - 1, 1)
            normalise(B - 1, 1)

        @block.tensor
        def _(pe):
            def parts(dst, hi, lo, x_hi, x_lo, first, last):
                pe.matmul(dst, hi, x_hi, start=first, stop=False)
                pe.matmul(dst, hi, x_lo, start=False, stop=False)
                return pe.matmul(dst, lo, x_hi, start=False, stop=last)

            def gate_up(b, n):
                q, e, ic = n // NP, n // DC % NE, n % DC
                if n % NP == 0 and not (isinstance(b, int) and b == 0 and q == 0):
                    pe.wait_ge(x_step, b * (2 * NH) + 2 * q)
                if not (isinstance(b, int) and b == 0 and n < 2):
                    pe.wait_ge(hf_ready, b * (NH * NP) + (n - 1))
                cols = slice(ic * P, (ic + 1) * P)
                for dst, j in ((psG[ic], WGT), (psU[ic], WUP)):
                    for c in range(DC):
                        last = parts(dst[:], w_hi[:, e, j, c, cols], w_lo[:, e, j, c, cols], x_hi[q][:, c, :], x_lo[q][:, c, :],
                                     c == 0, c == DC - 1)
                last.then_inc(gu_ready, 1)

            def down(b, q, e):
                pe.wait_ge(lo_ready, b * (NH * NP) + (q * NP + e * DC + DC))
                if e == 0 and not (isinstance(b, int) and b == 0 and q == 0):
                    pe.wait_ge(d_copied, b * (NH * DC) + q * DC)
                i = e % 2
                for oc in range(DC):
                    cols = slice(oc * P, (oc + 1) * P)
                    for ic in range(DC):
                        last = parts(psD[oc][:], w_hi[:, e, WDN, ic, cols], w_lo[:, e, WDN, ic, cols], h_hi[i][:, ic, :],
                                     h_lo[i][:, ic, :], e == 0 and ic == 0, e == NE - 1 and ic == DC - 1)
                last.then_inc(d_ready, 1)

            def to_rows(b, q):
                pe.wait_ge(d_copied, b * (NH * DC) + (q * DC + DC))
                if not (isinstance(b, int) and b == 0 and q == 0):
                    pe.wait_ge(acc_ready, b * (2 * NH) + 2 * q)
                for i in range(2):
                    for a in range(2):
                        s = 2 * i + a
                        for c in range(DC):
                            last = pe.transpose(psR[i][:, a * D + c * P:a * D + (c + 1) * P], dT[:, c, s * P:(s + 1) * P], ident[:])
                    last.then_inc(r_ready, 1)

            def body(b, first, last):
                for q in range(NH):
                    for e in range(NE):
                        n = q * NP + (e + 1) * DC
                        if not (last and n == NH * NP):
                            for ic in range(DC):
                                gate_up(b if n < NH * NP else b + 1, n % (NH * NP) + ic)
                        if e == 0 and not (first and q == 0):
                            to_rows(*before(b, q))
                        down(b, q, e)

            pe.wait_ge(const_ready, 5)
            for ic in range(DC):
                gate_up(0, ic)
            body(0, True, False)
            with pe.Fori(1, B - 1) as b:
                body(b, False, False)
            body(B - 1, False, True)
            to_rows(B - 1, 1)


def layer(nc, out, rope, x, Wq, bq, Wk, bk, Wv, bv, Wo, bo, w_ln1, w_ln2, W_kvd, W_qd, W_ku, W_qu, W_vu,
          W_ropeq, W_ropek, W_o, Wg_s, Wu_s, Wd_s, Wg_r, Wu_r, Wd_r, W_router, routing_bias):
    def scratch(name, shape, dt=F32):
        return nc.dram_tensor(name, shape, dt, kind="Internal").ap()

    x1, x12 = scratch("x1_rows", [B, S, D]), scratch("x1_x2_rows", [B, S, D])
    zd = scratch("z_rows", [HEADS, S])
    qp, kp = scratch("q_parts", [B, 3, D, S], BF16), scratch("k_parts", [B, 3, D, S], BF16)
    v_rows = scratch("v_rows", [B, S, MH * VW])
    y_cols = scratch("y_cols", [B, NH, NG, P, HALF])
    wt_rows = scratch("weight_rows", [NBLK, ER, HALF])
    xT2 = scratch("x2_norm_cols", [NBLK, P, DC, HALF])

    linear_attention(nc, x, Wq, bq, Wk, bk, Wv, bv, Wo, bo, x1, zd)
    latent_projections(nc, x1, w_ln1, W_kvd, W_qd, W_ku, W_qu, W_vu, W_ropeq, W_ropek, rope, qp, kp, v_rows)
    softmax_attention(nc, qp, kp, v_rows, y_cols)
    with ExitStack() as ctx:
        def parts(name, shape):
            return [ctx.enter_context(nc.sbuf_tensor(f"{name}_{part}", shape, F32R)) for part in ("hi", "lo")]

        w_hi, w_lo = parts("experts", [P, NE, 3, DC, D])
        x_hi, x_lo = zip(*(parts(f"x2_norm{i}", [P, DC, HALF]) for i in range(2)))
        output_and_router(nc, y_cols, x1, W_o, w_ln2, W_router, routing_bias, Wg_s, Wu_s, Wd_s, Wg_r, Wu_r, Wd_r,
                          x12, xT2, wt_rows, w_hi, w_lo, x_hi, x_lo)
        experts(nc, x12, xT2, wt_rows, w_hi, w_lo, x_hi, x_lo, out)


_ATTN = ["x", "Wq", "bq", "Wk", "bk", "Wv", "bv", "Wo", "bo"]
_FFN = ["w_ln1", "w_ln2", "W_kvd", "W_qd", "W_ku", "W_qu", "W_vu", "W_ropeq", "W_ropek", "W_o",
        "Wg_s", "Wu_s", "Wd_s", "Wg_r", "Wu_r", "Wd_r", "W_router", "routing_bias"]


def kernel(**inputs):
    import concourse.bacc as _bacc
    from concourse.bass_utils import run_bass_kernel_spmd as _run

    nc = _bacc.Bacc("TRN2", target_bir_lowering=False, num_devices=1)
    arrays = {"in_rope_dram": rope_table()}
    names = ["in_rope_dram"]
    for prefix, group in (("L0_attn_", _ATTN), ("L0_ffn_", _FFN)):
        for name in group:
            arrays[f"in_{prefix}{name}_dram"] = np.ascontiguousarray(inputs[prefix + name])
            names.append(f"in_{prefix}{name}_dram")
    args = [nc.dram_tensor("out_dram", (B, S, D), F32, kind="ExternalOutput").ap()]
    for name in names:
        a = arrays[name]
        args.append(nc.dram_tensor(name, a.shape, mybir.dt.from_np(a.dtype), kind="ExternalInput").ap())
    layer(nc, *args)
    r = _run(nc, [arrays], core_ids=[0])
    return r.results[0]["out_dram"]
```
